# Optimizing a Trainium2 kernel written in Bass

```python
import numpy as np
import jax
import jax.numpy as jnp

def _softmax(x, axis=-1):
    return jax.nn.softmax(x, axis=axis)

def _gelu(x):
    return jax.nn.gelu(x, approximate=True)

def _silu(x):
    return jax.nn.silu(x)

def _sigmoid(x):
    return jax.nn.sigmoid(x)

def _layernorm(x, axis=-1, eps=1e-05):
    m = jnp.mean(x, axis=axis, keepdims=True)
    v = jnp.var(x, axis=axis, keepdims=True)
    return (x - m) / jnp.sqrt(v + eps)

def _scatter_add(tgt, idx, src, axis=0):
    return tgt.at[idx].add(src)

def _segment_sum(src, seg, n):
    return jax.ops.segment_sum(src, seg, n)
kernel_name = 'mk_sandwich_d1_jaxref_r8_e93ccf'

def setup_inputs(seed: int=0):
    np.random.seed(seed)
    _w = jnp.asarray

    def _L0_attn_setup():
        import jax, jax.numpy as jnp
        import numpy as np
        import math
        EMBED_DIM = 128
        NUM_HEADS = 16
        HEAD_DIM = EMBED_DIM // NUM_HEADS
        WINDOW_SIZE = 32
        SCALING = math.sqrt(HEAD_DIM)
        key = jax.random.key(seed)
        ks = jax.random.split(key, 9)
        B, S, E = (2, 256, EMBED_DIM)
        s = 1.0 / math.sqrt(E)
        inp = {'hidden_states': jax.random.normal(ks[0], (B, S, E), dtype=jnp.float32), 'q_w': jax.random.uniform(ks[1], (E, E), jnp.float32, -s, s), 'q_b': jax.random.uniform(ks[2], (E,), jnp.float32, -s, s), 'k_w': jax.random.uniform(ks[3], (E, E), jnp.float32, -s, s), 'k_b': jax.random.uniform(ks[4], (E,), jnp.float32, -s, s), 'v_w': jax.random.uniform(ks[5], (E, E), jnp.float32, -s, s), 'v_b': jax.random.uniform(ks[6], (E,), jnp.float32, -s, s), 'o_w': jax.random.uniform(ks[7], (E, E), jnp.float32, -s, s), 'o_b': jax.random.uniform(ks[8], (E,), jnp.float32, -s, s)}
        return inp
    _L0_attn_in = _L0_attn_setup()

    def _L0_ffn_setup():
        import jax, jax.numpy as jnp
        import numpy as np
        DIM = 128
        DEPTH = 6
        HEADS = 16
        DIM_HEAD = 64
        WINDOW = 32
        INNER = HEADS * DIM_HEAD
        DIM_INNER = int(DIM * 4 * 2 / 3)
        QK_SCALE = 8.0

        def shift_tokens(t):
            a, s = jnp.split(t, 2, -1)
            s = jnp.pad(s, ((0, 0), (1, 0), (0, 0)))[:, :-1]
            return jnp.concatenate([a, s], -1)

        def l2norm(t):
            return t / jnp.maximum(jnp.linalg.norm(t, axis=-1, keepdims=True), 1e-12)

        def rotate_half(x):
            x1, x2 = jnp.split(x, 2, -1)
            return jnp.concatenate([-x2, x1], -1)

        def rotary_tables(n):
            half = jnp.arange(0, DIM_HEAD, 2, dtype=jnp.float32)
            inv_freq = 1.0 / 10000.0 ** (half / DIM_HEAD)
            t = jnp.arange(n, dtype=jnp.float32)
            freqs = t[:, None] * inv_freq[None, :]
            freqs = jnp.concatenate([freqs, freqs], -1)
            base_scale = (half + 0.4 * DIM_HEAD) / (1.4 * DIM_HEAD)
            power = (t - n // 2) / (WINDOW // 2)
            scale = base_scale[None, :] ** power[:, None]
            scale = jnp.concatenate([scale, scale], -1)
            return (freqs, scale)

        def local_attention(q, k, v):
            b, h, n, d = q.shape
            w = WINDOW
            nw = n // w
            bq = q.reshape(b, h, nw, w, d)
            bk = k.reshape(b, h, nw, w, d)
            bv = v.reshape(b, h, nw, w, d)

            def look(t):
                p = jnp.pad(t, ((0, 0), (0, 0), (1, 0), (0, 0), (0, 0)))
                return jnp.concatenate([p[:, :, :nw], p[:, :, 1:]], axis=3)
            bk2, bv2 = (look(bk), look(bv))
            seq = jnp.arange(n).reshape(nw, w)
            seq_p = jnp.pad(seq, ((1, 0), (0, 0)), constant_values=-1)
            jt = jnp.concatenate([seq_p[:nw], seq_p[1:]], axis=1)
            it = seq[:, :, None]
            jb = jt[:, None, :]
            mask = (it < jb) | (it > jb + w) | (jb == -1)
            sim = jnp.einsum('bhwie,bhwje->bhwij', bq, bk2) * QK_SCALE
            sim = jnp.where(mask, -jnp.finfo(sim.dtype).max, sim)
            attn = jax.nn.softmax(sim, -1)
            out = jnp.einsum('bhwij,bhwje->bhwie', attn, bv2)
            return out.reshape(b, h, n, d)

        def attn_layer(x, Wqkv, qs, ksc, Wo):
            b, n, _ = x.shape
            qkv = x @ Wqkv
            q, k, v = jnp.split(qkv, 3, -1)
            sh = lambda t: t.reshape(b, n, HEADS, DIM_HEAD).transpose(0, 2, 1, 3)
            q, k, v = (sh(q), sh(k), sh(v))
            q = l2norm(q) * qs
            k = l2norm(k) * ksc
            freqs, scale = rotary_tables(n)
            cos, sin = (jnp.cos(freqs), jnp.sin(freqs))
            q = q * cos * scale + rotate_half(q) * sin * scale
            inv = 1.0 / scale
            k = k * cos * inv + rotate_half(k) * sin * inv
            out = local_attention(q, k, v)
            out = out.transpose(0, 2, 1, 3).reshape(b, n, INNER)
            return out @ Wo

        def ffn_layer(x, g, bln, W1, b1, W2, b2):
            mu = x.mean(-1, keepdims=True)
            var = ((x - mu) ** 2).mean(-1, keepdims=True)
            xn = (x - mu) / jnp.sqrt(var + 1e-05) * g + bln
            hg = xn @ W1 + b1
            a, gate = jnp.split(hg, 2, -1)
            return a * jax.nn.gelu(gate, approximate=False) @ W2 + b2
        key = jax.random.key(seed)
        ks = jax.random.split(key, 8)
        B, N = (2, 256)
        init = lambda k, shape: jax.random.normal(k, shape, jnp.float32) * 0.02
        return {'x': jax.random.normal(ks[0], (B, N, DIM), jnp.float32), 'Wqkv': init(ks[1], (DEPTH, DIM, 3 * INNER)), 'q_scale': jnp.ones((DEPTH, DIM_HEAD), jnp.float32), 'k_scale': jnp.ones((DEPTH, DIM_HEAD), jnp.float32), 'Wo': init(ks[2], (DEPTH, INNER, DIM)), 'ln_g': jnp.ones((DEPTH, DIM), jnp.float32), 'ln_b': jnp.zeros((DEPTH, DIM), jnp.float32), 'W1': init(ks[3], (DEPTH, DIM, 2 * DIM_INNER)), 'b1': jnp.zeros((DEPTH, 2 * DIM_INNER), jnp.float32), 'W2': init(ks[4], (DEPTH, DIM_INNER, DIM)), 'b2': jnp.zeros((DEPTH, DIM), jnp.float32)}
    _L0_ffn_in = _L0_ffn_setup()
    _d = {'L0_attn_hidden_states': _L0_attn_in['hidden_states'], 'L0_attn_q_w': _L0_attn_in['q_w'], 'L0_attn_q_b': _L0_attn_in['q_b'], 'L0_attn_k_w': _L0_attn_in['k_w'], 'L0_attn_k_b': _L0_attn_in['k_b'], 'L0_attn_v_w': _L0_attn_in['v_w'], 'L0_attn_v_b': _L0_attn_in['v_b'], 'L0_attn_o_w': _L0_attn_in['o_w'], 'L0_attn_o_b': _L0_attn_in['o_b'], 'L0_ffn_Wqkv': _L0_ffn_in['Wqkv'], 'L0_ffn_q_scale': _L0_ffn_in['q_scale'], 'L0_ffn_k_scale': _L0_ffn_in['k_scale'], 'L0_ffn_Wo': _L0_ffn_in['Wo'], 'L0_ffn_ln_g': _L0_ffn_in['ln_g'], 'L0_ffn_ln_b': _L0_ffn_in['ln_b'], 'L0_ffn_W1': _L0_ffn_in['W1'], 'L0_ffn_b1': _L0_ffn_in['b1'], 'L0_ffn_W2': _L0_ffn_in['W2'], 'L0_ffn_b2': _L0_ffn_in['b2']}
    _x0 = _d['L0_attn_hidden_states']
    _d['L0_attn_hidden_states'] = jax.random.normal(jax.random.fold_in(jax.random.key(seed), 1), (2, 2048, 128), dtype=_x0.dtype)
    del _x0
    return _d

def reference(L0_attn_hidden_states, L0_attn_q_w, L0_attn_q_b, L0_attn_k_w, L0_attn_k_b, L0_attn_v_w, L0_attn_v_b, L0_attn_o_w, L0_attn_o_b, L0_ffn_Wqkv, L0_ffn_q_scale, L0_ffn_k_scale, L0_ffn_Wo, L0_ffn_ln_g, L0_ffn_ln_b, L0_ffn_W1, L0_ffn_b1, L0_ffn_W2, L0_ffn_b2):

    def _L0_attn_ref(hidden_states, q_w, q_b, k_w, k_b, v_w, v_b, o_w, o_b):
        import jax, jax.numpy as jnp
        import numpy as np
        import math
        EMBED_DIM = 128
        NUM_HEADS = 16
        HEAD_DIM = EMBED_DIM // NUM_HEADS
        WINDOW_SIZE = 32
        SCALING = math.sqrt(HEAD_DIM)
        B, S, E = hidden_states.shape
        H, D, w = (NUM_HEADS, HEAD_DIM, WINDOW_SIZE)
        W = 2 * w + 1
        q = hidden_states @ q_w.T + q_b
        k = hidden_states @ k_w.T + k_b
        v = hidden_states @ v_w.T + v_b
        q = q.reshape(B, S, H, D).transpose(0, 2, 1, 3)
        k = k.reshape(B, S, H, D).transpose(0, 2, 1, 3)
        v = v.reshape(B, S, H, D).transpose(0, 2, 1, 3)
        k_pad = jnp.pad(k, ((0, 0), (0, 0), (w, w), (0, 0)))
        v_pad = jnp.pad(v, ((0, 0), (0, 0), (w, w), (0, 0)))
        idx = jnp.arange(S)[:, None] + jnp.arange(W)[None, :]
        k_slice = k_pad[:, :, idx]
        v_slice = v_pad[:, :, idx]
        score = jnp.einsum('bhsd,bhswd->bhsw', q, k_slice) / SCALING
        p = jax.nn.softmax(score, axis=-1)
        attn = jnp.einsum('bhsw,bhswd->bhsd', p, v_slice)
        attn = attn.transpose(0, 2, 1, 3).reshape(B, S, E)
        return attn @ o_w.T + o_b

    def _L0_ffn_ref(x, Wqkv, q_scale, k_scale, Wo, ln_g, ln_b, W1, b1, W2, b2):
        import jax, jax.numpy as jnp
        import numpy as np
        DIM = 128
        DEPTH = 6
        HEADS = 16
        DIM_HEAD = 64
        WINDOW = 32
        INNER = HEADS * DIM_HEAD
        DIM_INNER = int(DIM * 4 * 2 / 3)
        QK_SCALE = 8.0

        def shift_tokens(t):
            a, s = jnp.split(t, 2, -1)
            s = jnp.pad(s, ((0, 0), (1, 0), (0, 0)))[:, :-1]
            return jnp.concatenate([a, s], -1)

        def l2norm(t):
            return t / jnp.maximum(jnp.linalg.norm(t, axis=-1, keepdims=True), 1e-12)

        def rotate_half(x):
            x1, x2 = jnp.split(x, 2, -1)
            return jnp.concatenate([-x2, x1], -1)

        def rotary_tables(n):
            half = jnp.arange(0, DIM_HEAD, 2, dtype=jnp.float32)
            inv_freq = 1.0 / 10000.0 ** (half / DIM_HEAD)
            t = jnp.arange(n, dtype=jnp.float32)
            freqs = t[:, None] * inv_freq[None, :]
            freqs = jnp.concatenate([freqs, freqs], -1)
            base_scale = (half + 0.4 * DIM_HEAD) / (1.4 * DIM_HEAD)
            power = (t - n // 2) / (WINDOW // 2)
            scale = base_scale[None, :] ** power[:, None]
            scale = jnp.concatenate([scale, scale], -1)
            return (freqs, scale)

        def local_attention(q, k, v):
            b, h, n, d = q.shape
            w = WINDOW
            nw = n // w
            bq = q.reshape(b, h, nw, w, d)
            bk = k.reshape(b, h, nw, w, d)
            bv = v.reshape(b, h, nw, w, d)

            def look(t):
                p = jnp.pad(t, ((0, 0), (0, 0), (1, 0), (0, 0), (0, 0)))
                return jnp.concatenate([p[:, :, :nw], p[:, :, 1:]], axis=3)
            bk2, bv2 = (look(bk), look(bv))
            seq = jnp.arange(n).reshape(nw, w)
            seq_p = jnp.pad(seq, ((1, 0), (0, 0)), constant_values=-1)
            jt = jnp.concatenate([seq_p[:nw], seq_p[1:]], axis=1)
            it = seq[:, :, None]
            jb = jt[:, None, :]
            mask = (it < jb) | (it > jb + w) | (jb == -1)
            sim = jnp.einsum('bhwie,bhwje->bhwij', bq, bk2) * QK_SCALE
            sim = jnp.where(mask, -jnp.finfo(sim.dtype).max, sim)
            attn = jax.nn.softmax(sim, -1)
            out = jnp.einsum('bhwij,bhwje->bhwie', attn, bv2)
            return out.reshape(b, h, n, d)

        def attn_layer(x, Wqkv, qs, ksc, Wo):
            b, n, _ = x.shape
            qkv = x @ Wqkv
            q, k, v = jnp.split(qkv, 3, -1)
            sh = lambda t: t.reshape(b, n, HEADS, DIM_HEAD).transpose(0, 2, 1, 3)
            q, k, v = (sh(q), sh(k), sh(v))
            q = l2norm(q) * qs
            k = l2norm(k) * ksc
            freqs, scale = rotary_tables(n)
            cos, sin = (jnp.cos(freqs), jnp.sin(freqs))
            q = q * cos * scale + rotate_half(q) * sin * scale
            inv = 1.0 / scale
            k = k * cos * inv + rotate_half(k) * sin * inv
            out = local_attention(q, k, v)
            out = out.transpose(0, 2, 1, 3).reshape(b, n, INNER)
            return out @ Wo

        def ffn_layer(x, g, bln, W1, b1, W2, b2):
            mu = x.mean(-1, keepdims=True)
            var = ((x - mu) ** 2).mean(-1, keepdims=True)
            xn = (x - mu) / jnp.sqrt(var + 1e-05) * g + bln
            hg = xn @ W1 + b1
            a, gate = jnp.split(hg, 2, -1)
            return a * jax.nn.gelu(gate, approximate=False) @ W2 + b2
        for i in range(DEPTH):
            x = attn_layer(shift_tokens(x), Wqkv[i], q_scale[i], k_scale[i], Wo[i]) + x
            x = ffn_layer(shift_tokens(x), ln_g[i], ln_b[i], W1[i], b1[i], W2[i], b2[i]) + x
        return x
    x = L0_attn_hidden_states
    x = x + _layernorm(_L0_attn_ref(_layernorm(x, axis=-1), L0_attn_q_w, L0_attn_q_b, L0_attn_k_w, L0_attn_k_b, L0_attn_v_w, L0_attn_v_b, L0_attn_o_w, L0_attn_o_b), axis=-1)
    x = x + _layernorm(_L0_ffn_ref(_layernorm(x, axis=-1), L0_ffn_Wqkv, L0_ffn_q_scale, L0_ffn_k_scale, L0_ffn_Wo, L0_ffn_ln_g, L0_ffn_ln_b, L0_ffn_W1, L0_ffn_b1, L0_ffn_W2, L0_ffn_b2), axis=-1)
    return x

_drawn_inputs = setup_inputs


def setup_inputs(seed=0):
    import zlib

    import numpy as np

    out = dict(_drawn_inputs(seed))
    spreads = {'L0_ffn_q_scale': (1.0, 0.6),
     'L0_ffn_k_scale': (1.0, 0.6),
     'L0_ffn_ln_g': (1.0, 0.6),
     'L0_ffn_ln_b': (0.0, 0.8),
     'L0_ffn_b1': (0.0, 0.8),
     'L0_ffn_b2': (0.0, 0.335)}
    factors = {'L0_attn_q_b': 3.691, 'L0_attn_k_b': 60.515, 'L0_ffn_W1': 4.495, 'L0_ffn_W2': 4.482}
    for name, (base, spread) in spreads.items():
        noise = np.random.default_rng([zlib.crc32(name.encode()), seed]).standard_normal(out[name].shape)
        drawn = base * np.exp(spread * noise) if base else spread * noise
        out[name] = jnp.asarray(drawn.astype(out[name].dtype))
    for name, factor in factors.items():
        out[name] = (out[name] * factor).astype(out[name].dtype)
    return out
```

```python
from contextlib import ExitStack

import numpy as np
import concourse.bass as bass
from concourse import mybir

F32 = mybir.dt.float32
BF16 = mybir.dt.bfloat16
I32 = mybir.dt.int32
ACT = mybir.ActivationFunctionType
ALU = mybir.AluOpType
AX_X = mybir.AxisListType.X

P = 128
BATCH, SEQ, E = 2, 2048, 128
LAYERS, HEADS, DH = 6, 16, 64
INNER = HEADS * DH
FF = 341
WIN = 32
BLK = 128
NBLK = BATCH * SEQ // BLK
PER_BATCH = SEQ // BLK
PAD = WIN + 1
WIDTH = BATCH * (PAD + SEQ) + WIN
CHUNK = 512
NCHUNK = BATCH * SEQ // CHUNK
HALF = 64
KEYS = WIN + HALF
KEYS_A = WIN + HALF + WIN
PAIRS = HEADS // 2
FF_TILES = [(0, 128), (128, 128), (256, FF - 256)]
QK_SCALE = 8.0
SCALE_A = 8.0 ** -0.5
STEPS = NBLK + 2
EPS_LN = 1e-5
CONST_LOADS = BATCH + 7
A_LOADS = 6
NORM_FLOOR = 1e-24
RSQRT_MAGIC = 0x5F3759DF


def block_col(i):
    return PAD + BLK * i + PAD * (i // PER_BATCH)


def chunk_col(c):
    return PAD + CHUNK * c + PAD * (c // (SEQ // CHUNK))


def pipeline(eng, step):
    step(0, 0, True, False, False, 0)
    step(1, 1, True, True, False, 1)
    with eng.Fori(0, (NBLK - 2) // 2) as k:
        step(2 * k + 2, 0, True, True, True, 2)
        step(2 * k + 3, 1, True, True, True, 3)
    step(NBLK, 0, False, True, True, NBLK)
    step(NBLK + 1, 1, False, False, True, NBLK + 1)


def program(nc, d):
    with ExitStack() as ctx:
        def sb(name, shape, dt=F32):
            return ctx.enter_context(nc.sbuf_tensor(name, shape, dt))

        def psum(name, shape):
            return ctx.enter_context(nc.psum_tensor(name, shape, F32))

        def sem(name):
            return ctx.enter_context(nc.semaphore(name))

        X = sb("X", [P, WIDTH])
        N = sb("N", [P, WIDTH])
        Y = sb("Y", [P, WIDTH])
        Y2 = sb("Y2", [P, WIDTH])
        tab = sb("tab", [P, PER_BATCH * 4 * DH])
        center = sb("center", [P, P])
        mean_of = sb("mean_of", [P, P])
        ident = sb("ident", [P, P])
        ident_bf = sb("ident_bf", [P, P], BF16)
        mask_b = sb("mask_b", [P, NBLK * KEYS], BF16)
        mask_a = sb("mask_a", [P, KEYS_A], BF16)
        eps_col = sb("eps_col", [P, 1])
        one_col = sb("one_col", [P, 1])
        keep = sb("keep", [P, NBLK])
        wqkv = sb("wqkv", [P, 3 * INNER])
        wo = sb("wo", [P, PAIRS, P])
        w1 = sb("w1", [P, 2 * FF])
        w2 = sb("w2", [P, len(FF_TILES), P])
        vec = sb("vec", [P, 9])
        qk_scales = sb("qk_scales", [P, 4 * DH])
        xs = sb("xs", [P, 2, WIN + BLK])
        ts = sb("ts", [P, 2, 4, DH])
        u = sb("u", [P, 4, 512])
        sq = sb("sq", [P, 4, 512])
        t1 = sb("t1", [P, 4, 512])
        t2 = sb("t2", [P, 4, 512])
        ss = sb("ss", [P, 4, 8])
        rn = sb("rn", [P, 4, 8])
        rt = sb("rt", [P, 4, 8])
        qT = sb("qT", [P, PAIRS, BLK])
        kW = sb("kW", [P, 2, PAIRS, WIN + BLK])
        pr = sb("pr", [P, 2 * PAIRS, KEYS])
        pT = sb("pT", [P, 2 * PAIRS, P])
        vW = sb("vW", [P, 2, 2, INNER])
        oT = sb("oT", [P, PAIRS, BLK])
        mx = sb("mx", [P, 16])
        nbias = sb("nbias", [P, 16])
        rsum = sb("rsum", [P, 16])
        rrec = sb("rrec", [P, 16])
        a_w = wqkv[:, 0:384]
        a_wo = wqkv[:, 384:896].rearrange("p (a n) -> p a n", a=4)
        a_bias = wqkv[0:1, 896:1280]
        a_ob = wqkv[:, 1280:1281]
        a_heads = wqkv[:, 1282:1298]
        a_x = t2[:, 0, 0:384].rearrange("p (b n) -> p b n", b=2)
        a_valid = t2[0:1, 1, 0:384].rearrange("p (b n) -> p b n", b=2)
        a_ok = Y[0:1, 0:WIDTH]
        a_q = u[:, :, :].rearrange("p a (b n) -> p (a b) n", n=BLK)
        a_qk = oT[:, :, :].rearrange("p a n -> p (a n)")[:, 0:2 * (BLK + 192)].rearrange("p (b n) -> p b n", b=2)
        a_v = t2[:, 3, 0:512].rearrange("p (b w n) -> p b w n", b=2, w=2)
        a_p = t1[:, :, :].rearrange("p a (b n) -> p (a b) n", n=KEYS_A)
        a_on = sq[:, 0, 0:128].rearrange("p (w n) -> p w n", w=2)
        a_oT = sq[:, 1, 0:128]
        masks_in = vW[:, :, :, :].rearrange("p b w n -> p (b w n)")[:, 0:NBLK * KEYS + KEYS_A]
        ln_x = u[:, 0:2, :]
        ln_sq = sq[:, 0:2, :]
        ln_sd = t1[:, 0:2, :]
        ln_rs = t2[:, 0:2, :]
        ln_o = pT[:, 0:8, :].rearrange("p (b a) n -> p b (a n)", b=2)
        gelu = (u, sq)
        hid = (t1, t2)

        pj = [psum("pj0", [P, 512]), psum("pj1", [P, 512])]
        tr = [psum("tr0", [P, 512]), psum("tr1", [P, 512])]
        sc = [psum("sc0", [P, 512]), psum("sc1", [P, 512])]
        po = psum("po", [P, 512])
        py = psum("py", [P, 512])

        gate_banks = (pj[0], tr[0], sc[0])
        linear_banks = (pj[1], tr[1], sc[1])

        bar = sem("bar")
        attn_over = sem("attn_over")
        norm_over = sem("norm_over")
        ffn_over = sem("ffn_over")
        in_const = sem("in_const")
        in_a = sem("in_a")
        in_attn = sem("in_attn")
        in_ffn = sem("in_ffn")
        zeroed = sem("zeroed")
        stored = sem("stored")
        ln_staged = sem("ln_staged")
        ln_centered = sem("ln_centered")
        ln_squared = sem("ln_squared")
        ln_var = sem("ln_var")
        ln_rooted = sem("ln_rooted")
        ln_rec = sem("ln_rec")
        ln_scaled = sem("ln_scaled")
        ln_done = sem("ln_done")
        a_staged = sem("a_staged")
        a_qk_ready = sem("a_qk_ready")
        a_qk_copied = sem("a_qk_copied")
        a_q_ready = sem("a_q_ready")
        a_v_ready = sem("a_v_ready")
        a_v_copied = sem("a_v_copied")
        a_scored = sem("a_scored")
        a_max_chain = sem("a_max_chain")
        a_max_ready = sem("a_max_ready")
        a_exp_done = sem("a_exp_done")
        a_pT_ready = sem("a_pT_ready")
        a_pT_copied = sem("a_pT_copied")
        a_pv_done = sem("a_pv_done")
        a_rec_ready = sem("a_rec_ready")
        a_o_scaled = sem("a_o_scaled")
        a_oT_ready = sem("a_oT_ready")
        a_oT_copied = sem("a_oT_copied")
        a_y_ready = sem("a_y_ready")
        a_y_done = sem("a_y_done")
        xs_ready = sem("xs_ready")
        ts_ready = sem("ts_ready")
        qk_ready = sem("qk_ready")
        qk_copied = sem("qk_copied")
        sq_ready = sem("sq_ready")
        ss_ready = sem("ss_ready")
        rn_chain = sem("rn_chain")
        un_ready = sem("un_ready")
        t1_ready = sem("t1_ready")
        t2_ready = sem("t2_ready")
        qkT_ready = sem("qkT_ready")
        qkT_copied = sem("qkT_copied")
        v_ready = sem("v_ready")
        v_copied = sem("v_copied")
        scored = sem("scored")
        max_chain = sem("max_chain")
        max_ready = sem("max_ready")
        exp_done = sem("exp_done")
        rec_ready = sem("rec_ready")
        p_scaled = sem("p_scaled")
        pT_ready = sem("pT_ready")
        pT_copied = sem("pT_copied")
        pv_done = sem("pv_done")
        o_copied = sem("o_copied")
        y_ready = sem("y_ready")
        y_done = sem("y_done")
        h_ready = sem("h_ready")
        gelu_done = sem("gelu_done")
        hid_ready = sem("hid_ready")
        f_ready = sem("f_ready")
        f_done = sem("f_done")

        def staged_copy(pool, rows, dst, src):
            return pool.tensor_tensor(dst, src, one_col[rows, 0:1].broadcast_to([HALF, WIN + BLK]), ALU.mult)

        def barrier(eng, k):
            eng.drain().then_inc(bar, 1)
            eng.wait_ge(bar, 4 * k)

        def over(eng, phase):
            eng.drain().then_inc(phase, 1)

        block = ctx.enter_context(nc.Block())

        @block.sync
        def _(sp):
            for b in range(BATCH):
                at = PAD + b * (PAD + SEQ)
                sp.dma_start(X[:, at:at + SEQ], d["x"][:, b * SEQ:(b + 1) * SEQ]).then_inc(in_const, 16)
            for dst, src in ((center, "center"), (mean_of, "mean_of"), (ident, "ident"), (masks_in, "masks"),
                             (eps_col, "eps_col"), (keep, "keep")):
                sp.dma_start(dst[:, :], d[src]).then_inc(in_const, 16)
            sp.wait_ge(zeroed, 1)
            for dst, src in ((a_w, "a_w"), (a_bias, "a_bias"), (a_ob, "a_ob"), (a_heads, "a_heads"), (a_ok, "a_ok")):
                sp.dma_start(dst, d[src]).then_inc(in_a, 16)
            sp.dma_start(a_wo, d["a_wo"].rearrange("a p n -> p a n")).then_inc(in_a, 16)
            sp.dma_start(tab[:, :], d["tab"]).then_inc(in_const, 16)

            def load_ffn(n):
                sp.dma_start(w1[:, :], d["w1"][n]).then_inc(in_ffn, 16)
                sp.dma_start(w2[:, :, :], d["w2"][n].rearrange("(t p) n -> p t n", p=P)).then_inc(in_ffn, 16)
                sp.dma_start(vec[:, :], d["vec"][n]).then_inc(in_ffn, 16)

            def load_attn(n):
                sp.dma_start(wqkv[:, :], d["wqkv"][n]).then_inc(in_attn, 16)
                sp.dma_start(wo[:, :, :], d["wo"][n].rearrange("(t p) n -> p t n", p=P)).then_inc(in_attn, 16)
                sp.dma_start(qk_scales[:, :], d["qk_scales"][n].partition_broadcast(P)).then_inc(in_attn, 16)

            load_ffn(0)
            sp.wait_ge(bar, 4 * 3)
            load_attn(0)
            with sp.Fori(0, LAYERS - 1) as n:
                sp.wait_ge(attn_over, 4 * n + 4)
                load_attn(n + 1)
                sp.wait_ge(ffn_over, 3 * n + 6)
                load_ffn(n + 1)
            sp.wait_ge(ln_done, 2 * NCHUNK + 2)
            for b in range(BATCH):
                at = PAD + b * (PAD + SEQ)
                sp.dma_start(d["out"][:, b * SEQ:(b + 1) * SEQ], X[:, at:at + SEQ]).then_inc(stored, 16)
            sp.wait_ge(stored, 16 * BATCH)

        @block.gpsimd
        def _(pool):
            def layer_norm(src, run, shifted, L=None):
                with pool.Fori(0, NCHUNK // 2) as k:
                    if L is not None:
                        pool.wait_ge(attn_over, 4 * L + 4)
                    for h in range(2):
                        c = 2 * k + h
                        at = chunk_col(c)
                        pool.wait_ge(ln_centered, NCHUNK * run + c + 1)
                        pool.tensor_copy(ln_x[0:64, h, :], src[0:64, bass.ds(at, CHUNK)]).then_inc(ln_staged, 1)
                        late = 1 if shifted else 0
                        pool.tensor_copy(ln_x[64:128, h, :],
                                         src[64:128, bass.ds(at - late, CHUNK)]).then_inc(ln_staged, 1)

            def layer_norm_add(src, run, add_run, last=False):
                def add(c, h):
                    at = chunk_col(c)
                    pool.wait_ge(ln_scaled, NCHUNK * run + c + 3)
                    pool.tensor_tensor(X[:, bass.ds(at, CHUNK)], X[:, bass.ds(at, CHUNK)], ln_o[:, h, :],
                                       ALU.add).then_inc(ln_done, 1)

                with pool.Fori(0, NCHUNK // 2) as k:
                    if last:
                        pool.wait_ge(ffn_over, 3 * LAYERS + 3)
                    pool.wait_ge(ln_done, NCHUNK * add_run + 2 * k + 2)
                    for h in range(2):
                        c = 2 * k + h
                        pool.wait_ge(ln_centered, NCHUNK * run + c + 1)
                        pool.tensor_copy(ln_x[0:64, h, :],
                                         src[0:64, bass.ds(chunk_col(c), CHUNK)]).then_inc(ln_staged, 1)
                        pool.tensor_copy(ln_x[64:128, h, :],
                                         src[64:128, bass.ds(chunk_col(c), CHUNK)]).then_inc(ln_staged, 1)
                    pool.wait_ge(ln_staged, 2 * (NCHUNK * run + 2 * k + 2))
                    for h in range(2):
                        add(2 * k + h, h)

            def step_a(s, par, front, mid, back, since):
                if front:
                    at = block_col(s) - WIN
                    if since >= 2:
                        pool.wait_ge(a_v_ready, s - 1)
                    pool.tensor_copy(a_x[:, par, :], N[:, bass.ds(at, KEYS_A + HALF)]).then_inc(a_staged, 1)
                    pool.tensor_copy(a_valid[:, par, :], a_ok[:, bass.ds(at, KEYS_A + HALF)]).then_inc(a_staged, 1)

            def step_b(base, s, par, front, mid, back, since):
                g = base + s
                if front:
                    at = block_col(s) - WIN
                    if since >= 2:
                        pool.wait_ge(v_ready, 4 * g - 4)
                        pool.wait_ge(t2_ready, 4 * g - 4)
                    if since >= 1:
                        pool.wait_ge(t1_ready, 4 * g)
                    staged_copy(pool, slice(0, 64), xs[0:64, par, :], Y[0:64, bass.ds(at, WIN + BLK)]).then_inc(xs_ready, 1)
                    staged_copy(pool, slice(64, 128), xs[64:128, par, :], Y[64:128, bass.ds(at - 1, WIN + BLK)]).then_inc(xs_ready, 1)
                    pool.wait_ge(xs_ready, 2 * g + 2)
                    pool.tensor_tensor(ts[:, par, :, :].rearrange("p t d -> p (t d)"),
                                       tab[:, bass.ds((s % PER_BATCH) * 4 * DH, 4 * DH)],
                                       qk_scales[:, :], ALU.mult).then_inc(ts_ready, 1)
                if back:
                    for j in range(4):
                        pool.wait_ge(rec_ready, 4 * g + j - 7)
                        pool.tensor_tensor(pr[:, 4 * j:4 * j + 4, :], pr[:, 4 * j:4 * j + 4, :],
                                           rrec[:, 4 * j:4 * j + 4].unsqueeze(2).broadcast_to([P, 4, KEYS]),
                                           ALU.mult).then_inc(p_scaled, 1)
                if front:
                    pool.wait_ge(ts_ready, g + 1)
                    for n in range(4):
                        pool.wait_ge(un_ready, 4 * g + n + 1)
                        if since >= 1:
                            pool.wait_ge(qkT_ready, 4 * g + n - 3)
                        table = ts[:, par, 2 * (n // 2), :].unsqueeze(1).broadcast_to([P, 8, DH])
                        pool.tensor_tensor(t1[:, n, :].rearrange("p (h d) -> p h d", d=DH),
                                           u[:, n, :].rearrange("p (h d) -> p h d", d=DH), table,
                                           ALU.mult).then_inc(t1_ready, 1)

            pool.memset(one_col[:, :], 1.0)
            pool.memset(N[:, :], 0.0)
            pool.memset(Y2[:, :], 0.0)
            pool.memset(kW[:, :, :, :].rearrange("p b h n -> p (b h n)"), 0.0)
            barrier(pool, 1)
            pool.wait_ge(in_const, 16 * CONST_LOADS)
            layer_norm(X, 0, False)
            barrier(pool, 2)
            pool.wait_ge(in_a, 16 * A_LOADS)
            pipeline(pool, step_a)
            barrier(pool, 3)
            layer_norm_add(Y2, 1, 0)
            barrier(pool, 4)
            layer_norm(X, 2, False)
            with pool.Fori(0, LAYERS) as L:
                pool.wait_ge(ffn_over, 3 * L + 3)
                pool.wait_ge(in_attn, 48 * L + 48)
                pipeline(pool, lambda *a: step_b(NBLK * L, *a))
                over(pool, attn_over)
                layer_norm(Y2, L + 3, True, L)
                over(pool, norm_over)
            layer_norm_add(Y, 3 + LAYERS, 1, last=True)

        @block.scalar
        def _(act):
            def layer_norm(run, L=None):
                with act.Fori(0, NCHUNK // 2) as k:
                    if L is not None:
                        act.wait_ge(attn_over, 4 * L + 4)
                        act.wait_ge(in_ffn, 48 * L + 48)
                    for h in range(2):
                        n = NCHUNK * run + 2 * k + h
                        act.wait_ge(ln_centered, n + 3)
                        act.wait_ge(ln_var, n + 1)
                        act.activation(ln_sq[:, h, :], pj[h][:, :], ACT.Square).then_inc(ln_squared, 1)
                    for h in range(2):
                        n = NCHUNK * run + 2 * k + h
                        act.wait_ge(ln_var, n + 3)
                        act.wait_ge(ln_rec, n + 1)
                        act.activation(ln_sd[:, h, :], tr[h][:, :], ACT.Sqrt,
                                       bias=eps_col[:, 0:1]).then_inc(ln_rooted, 1)

            def step_a(s, par, front, mid, back, since):
                def turned(j):
                    act.wait_ge(a_pT_ready, 4 * s + j - 7)
                    act.copy(pT[:, 4 * j:4 * j + 4, :].rearrange("p a n -> p (a n)"),
                             tr[j % 2][:, :]).then_inc(a_pT_copied, 1)

                def exponentials(j):
                    act.wait_ge(a_max_ready, 4 * s + j - 3)
                    for p in range(4):
                        last = act.activation(a_p[:, 4 * j + p, :], sc[j % 2][:, p * KEYS_A:(p + 1) * KEYS_A],
                                              ACT.Exp, bias=nbias[:, 4 * j + p:4 * j + p + 1], scale=SCALE_A,
                                              accum_out=rsum[:, 4 * j + p:4 * j + p + 1])
                    last.then_inc(a_exp_done, 1)

                if front:
                    act.wait_ge(a_qk_ready, s + 1)
                    act.copy(a_qk[:, par, :], pj[0][:, 0:BLK + 192]).then_inc(a_qk_copied, 1)
                if back:
                    turned(0)
                    turned(1)
                if mid:
                    if since >= 2:
                        act.wait_ge(a_rec_ready, s - 1)
                    exponentials(0)
                if back:
                    turned(2)
                    turned(3)
                if mid:
                    exponentials(1)
                    act.wait_ge(a_v_ready, s)
                    act.copy(a_v[:, 1 - par, :, :].rearrange("p w n -> p (w n)"),
                             pj[1][:, 0:256]).then_inc(a_v_copied, 1)
                    exponentials(2)
                if back:
                    act.wait_ge(a_oT_ready, s - 1)
                    act.copy(a_oT, py[:, 256:384]).then_inc(a_oT_copied, 1)
                if mid:
                    exponentials(3)
                if back:
                    act.wait_ge(a_y_ready, s - 1)
                    act.activation(Y2[:, bass.ds(block_col(s - 2), BLK)], py[:, 0:BLK], ACT.Identity,
                                   bias=a_ob).then_inc(a_y_done, 1)

            def step_b(base, s, par, front, mid, back, since):
                g = base + s

                def projected(n):
                    act.wait_ge(qk_ready, 4 * g + n + 1)
                    if since >= 1:
                        act.wait_ge(t1_ready, 4 * g + n - 3)
                        act.wait_ge(t2_ready, 4 * g + n - 3)
                    act.copy(u[:, n, :], pj[n % 2][:, :])
                    act.activation(sq[:, n, :], pj[n % 2][:, :], ACT.Square).then_inc(qk_copied, 1)

                def turned(n):
                    act.wait_ge(qkT_ready, 4 * g + n - 3)
                    bank = tr[n % 2][:, :].rearrange("p (a n) -> p a n", n=BLK)
                    half = 4 * (n % 2)
                    if n < 2:
                        last = act.copy(qT[:, half:half + 4, :], bank)
                    else:
                        act.copy(kW[:, 1 - par, half:half + 4, WIN:WIN + BLK], bank)
                        last = act.activation(kW[:, par, half:half + 4, 0:WIN], bank[:, :, BLK - WIN:BLK],
                                              ACT.Identity, scale=keep[:, bass.ds(s - 1, 1)])
                    last.then_inc(qkT_copied, 1)

                def turned_p(j):
                    act.wait_ge(pT_ready, 4 * g + j - 7)
                    act.copy(pT[0:KEYS, 4 * j:4 * j + 4, :].rearrange("p a n -> p (a n)"),
                             tr[j % 2][0:KEYS, :]).then_inc(pT_copied, 1)

                def exponentials(j):
                    act.wait_ge(max_ready, 4 * g + j - 3)
                    for p in range(4):
                        last = act.activation(pr[:, 4 * j + p, :], sc[j % 2][:, p * KEYS:(p + 1) * KEYS],
                                              ACT.Exp, bias=nbias[:, 4 * j + p:4 * j + p + 1], scale=QK_SCALE,
                                              accum_out=rsum[:, 4 * j + p:4 * j + p + 1])
                    last.then_inc(exp_done, 1)

                def outputs(w):
                    act.wait_ge(pv_done, 2 * g + w - 3)
                    act.copy(oT[:, :, HALF * w:HALF * w + HALF],
                             po[:, :].rearrange("p (a n) -> p a n", n=HALF)).then_inc(o_copied, 1)

                for n in (0, 2):
                    if front:
                        projected(n)
                        projected(n + 1)
                    if mid:
                        turned(n)
                        turned(n + 1)
                if back:
                    turned_p(0)
                    turned_p(1)
                    turned_p(2)
                if mid:
                    exponentials(0)
                if back:
                    turned_p(3)
                if mid:
                    exponentials(1)
                for w in range(2):
                    if back:
                        outputs(w)
                    if mid:
                        exponentials(2 + w)

            def feed_forward(L):
                with act.Fori(0, NCHUNK // 2) as k:
                    act.wait_ge(norm_over, 4 * L + 4)
                    for h in range(2):
                        n = NCHUNK * L + 2 * k + h
                        for t, (_, m) in enumerate(FF_TILES):
                            act.wait_ge(h_ready, 6 * n + 2 * t + 1)
                            act.activation(gelu[h][0:m, t, :], gate_banks[t][0:m, :], ACT.Gelu,
                                           bias=vec[0:m, t:t + 1]).then_inc(gelu_done, 1)

            act.sem_inc(ln_rooted, 2)
            act.sem_inc(gelu_done, len(FF_TILES))
            barrier(act, 1)
            act.wait_ge(in_const, 16 * CONST_LOADS)
            layer_norm(0)
            barrier(act, 2)
            act.wait_ge(in_a, 16 * A_LOADS)
            pipeline(act, step_a)
            barrier(act, 3)
            layer_norm(1)
            barrier(act, 4)
            layer_norm(2)
            over(act, ffn_over)
            with act.Fori(0, LAYERS) as L:
                act.wait_ge(ffn_over, 3 * L + 3)
                pipeline(act, lambda *a: step_b(NBLK * L, *a))
                over(act, attn_over)
                layer_norm(L + 3, L)
                over(act, norm_over)
                feed_forward(L)
                over(act, ffn_over)
            act.wait_ge(ffn_over, 3 * LAYERS + 3)
            layer_norm(3 + LAYERS)

        @block.vector
        def _(dve):
            def layer_norm(run, dst, affine=False, add_run=None, L=None):
                with dve.Fori(0, NCHUNK // 2) as k:
                    if L is not None:
                        dve.wait_ge(attn_over, 4 * L + 4)
                        dve.wait_ge(in_ffn, 48 * L + 48)
                    for h in range(2):
                        c = 2 * k + h
                        n = NCHUNK * run + c
                        at = chunk_col(c)
                        dve.wait_ge(ln_rooted, n + 3)
                        dve.reciprocal(ln_rs[:, h, :], ln_sd[:, h, :]).then_inc(ln_rec, 1)
                        if add_run is not None:
                            dve.wait_ge(ln_done, NCHUNK * add_run + c + 1)
                        out = ln_o[:, h, :] if affine or add_run is not None else dst[:, bass.ds(at, CHUNK)]
                        dve.wait_ge(ln_rec, n + 3)
                        dve.tensor_tensor(out, pj[h][:, :], ln_rs[:, h, :], ALU.mult).then_inc(ln_scaled, 1)
                        if affine:
                            dve.wait_ge(ln_scaled, n + 3)
                            dve.tensor_scalar(dst[:, bass.ds(at, CHUNK)], ln_o[:, h, :], vec[:, 7:8], vec[:, 8:9],
                                              ALU.mult, ALU.add)

            def step_a(s, par, front, mid, back, since):
                def maxima(j):
                    dve.wait_ge(a_scored, 4 * s + j - 3)
                    dve.reduce_max(mx[:, 4 * j:4 * j + 4], sc[j % 2][:, :].rearrange("p (a n) -> p a n", n=KEYS_A),
                                   axis=AX_X).then_inc(a_max_chain, 1)
                    dve.wait_ge(a_max_chain, 4 * s + j - 3)
                    dve.tensor_scalar(nbias[:, 4 * j:4 * j + 4], mx[:, 4 * j:4 * j + 4], -SCALE_A, None,
                                      ALU.mult).then_inc(a_max_ready, 1)

                def spread(w):
                    at = slice(HALF * w, HALF * w + HALF)
                    dve.tensor_tensor(a_q[:, :, at], a_qk[:, par, at].unsqueeze(1).broadcast_to([P, HEADS, HALF]),
                                      a_heads.unsqueeze(2).broadcast_to([P, HEADS, HALF]),
                                      ALU.mult).then_inc(a_q_ready, 1)

                if back:
                    dve.wait_ge(a_exp_done, 4 * s - 4)
                    dve.reciprocal(rrec[:, :], rsum[:, :]).then_inc(a_rec_ready, 1)
                if mid:
                    maxima(0)
                    maxima(1)
                if front:
                    dve.wait_ge(a_qk_copied, s + 1)
                    spread(0)
                if back:
                    dve.wait_ge(a_pv_done, s - 1)
                    dve.wait_ge(a_rec_ready, s - 1)
                    dve.tensor_tensor(a_on.rearrange("p w (a d) -> p (w a) d", d=8),
                                      po[:, 0:128].rearrange("p (a d) -> p a d", d=8),
                                      rrec[:, :].unsqueeze(2).broadcast_to([P, 16, 8]),
                                      ALU.mult).then_inc(a_o_scaled, 1)
                if mid:
                    maxima(2)
                    maxima(3)
                if front:
                    spread(1)

            CHAIN = 12

            def step_b(base, s, par, front, mid, back, since):
                g = base + s

                def values(n):
                    dve.wait_ge(v_ready, 4 * g + n - 3)
                    dve.tensor_copy(vW[0:KEYS, 1 - par, n // 2, 512 * (n % 2):512 * (n % 2) + 512],
                                    pj[n % 2][0:KEYS, :]).then_inc(v_copied, 1)

                def second_term(n):
                    dve.wait_ge(un_ready, 4 * g + n + 1)
                    if since >= 1:
                        dve.wait_ge(qkT_ready, 4 * g + n - 3)
                    if n == 0:
                        dve.wait_ge(ts_ready, g + 1)
                    src = u[:, n, :].rearrange("p (h d) -> p h d", d=DH)
                    dst = t2[:, n, :].rearrange("p (h d) -> p h d", d=DH)
                    table = ts[:, par, 2 * (n // 2) + 1, :].unsqueeze(1).broadcast_to([P, 8, DH])
                    dve.tensor_tensor(dst[:, :, 0:32], src[:, :, 32:64], table[:, :, 0:32], ALU.mult)
                    dve.tensor_tensor(dst[:, :, 32:64], src[:, :, 0:32], table[:, :, 32:64],
                                      ALU.mult).then_inc(t2_ready, 1)

                def maxima(j):
                    dve.wait_ge(scored, 4 * g + j - 3)
                    dve.reduce_max(mx[:, 4 * j:4 * j + 4],
                                   sc[j % 2][:, 0:4 * KEYS].rearrange("p (a n) -> p a n", n=KEYS),
                                   axis=AX_X).then_inc(max_chain, 1)
                    dve.wait_ge(max_chain, 4 * g + j - 3)
                    dve.tensor_scalar(nbias[:, 4 * j:4 * j + 4], mx[:, 4 * j:4 * j + 4], -QK_SCALE, None,
                                      ALU.mult).then_inc(max_ready, 1)

                def sums(j):
                    dve.wait_ge(exp_done, 4 * g + j - 3)
                    dve.reciprocal(rrec[:, 4 * j:4 * j + 4], rsum[:, 4 * j:4 * j + 4]).then_inc(rec_ready, 1)

                if front:
                    for n in range(4):
                        dve.wait_ge(qk_copied, 4 * g + n + 1)
                        dve.reduce_sum(ss[:, n, :], sq[:, n, :].rearrange("p (h d) -> p h d", d=DH),
                                       axis=AX_X).then_inc(ss_ready, 1)
                    all_ss = ss[:, :, :].rearrange("p a b -> p (a b)")
                    y = rn[:, :, :].rearrange("p a b -> p (a b)")
                    t = rt[:, :, :].rearrange("p a b -> p (a b)")
                    dve.wait_ge(ss_ready, 4 * g + 4)
                    dve.tensor_scalar(all_ss, all_ss, NORM_FLOOR, None, ALU.max).then_inc(rn_chain, 1)
                    dve.wait_ge(rn_chain, CHAIN * g + 1)
                    dve.tensor_scalar(t.bitcast(I32), all_ss.bitcast(I32), 1, None,
                                      ALU.logical_shift_right).then_inc(rn_chain, 1)
                    dve.wait_ge(rn_chain, CHAIN * g + 2)
                    dve.tensor_scalar(y.bitcast(I32), t.bitcast(I32), -1.0, float(RSQRT_MAGIC), ALU.mult,
                                      ALU.add).then_inc(rn_chain, 1)
                    for r in range(3):
                        dve.wait_ge(rn_chain, CHAIN * g + 3 * r + 3)
                        dve.scalar_tensor_tensor(t, y, -0.5, y, ALU.mult, ALU.mult).then_inc(rn_chain, 1)
                        dve.wait_ge(rn_chain, CHAIN * g + 3 * r + 4)
                        dve.tensor_tensor(t, t, all_ss, ALU.mult).then_inc(rn_chain, 1)
                        dve.wait_ge(rn_chain, CHAIN * g + 3 * r + 5)
                        dve.scalar_tensor_tensor(y, t, 1.5, y, ALU.add, ALU.mult).then_inc(rn_chain, 1)
                    dve.wait_ge(rn_chain, CHAIN * g + CHAIN)
                for n in range(4):
                    if front:
                        dve.tensor_tensor(u[:, n, :].rearrange("p (h d) -> p h d", d=DH),
                                          u[:, n, :].rearrange("p (h d) -> p h d", d=DH),
                                          rn[:, n, :].unsqueeze(2).broadcast_to([P, 8, DH]),
                                          ALU.mult).then_inc(un_ready, 1)
                    if mid and n < 2:
                        maxima(n)
                if mid:
                    values(0)
                    values(1)
                    maxima(2)
                if front:
                    second_term(0)
                if mid:
                    values(2)
                    values(3)
                if front:
                    second_term(1)
                if mid:
                    sums(0)
                    sums(1)
                    maxima(3)
                if front:
                    second_term(2)
                    second_term(3)
                if mid:
                    sums(2)
                    sums(3)
                if back:
                    at = block_col(s - 2)
                    dve.wait_ge(y_ready, g - 1)
                    dve.tensor_tensor(Y2[:, bass.ds(at, BLK)], py[:, 0:BLK], Y[:, bass.ds(at, BLK)],
                                      ALU.add).then_inc(y_done, 1)

            def feed_forward(L):
                with dve.Fori(0, NCHUNK // 2) as k:
                    dve.wait_ge(norm_over, 4 * L + 4)
                    for h in range(2):
                        n = NCHUNK * L + 2 * k + h
                        for t, (_, m) in enumerate(FF_TILES):
                            dve.wait_ge(h_ready, 6 * n + 2 * t + 2)
                            dve.wait_ge(gelu_done, 3 * n + t + 4)
                            dve.scalar_tensor_tensor(hid[h][0:m, t, :], linear_banks[t][0:m, :],
                                                     vec[0:m, 3 + t:4 + t], gelu[h][0:m, t, :],
                                                     ALU.add, ALU.mult).then_inc(hid_ready, 1)
                    for h in range(2):
                        c = 2 * k + h
                        at = chunk_col(c)
                        dve.wait_ge(f_ready, NCHUNK * L + c + 1)
                        dve.scalar_tensor_tensor(Y[:, bass.ds(at, CHUNK)], (po, py)[h][:, :], vec[:, 6:7],
                                                 Y2[:, bass.ds(at, CHUNK)], ALU.add, ALU.add).then_inc(f_done, 1)

            dve.memset(Y[:, :], 0.0).then_inc(zeroed, 1)
            dve.sem_inc(ln_rec, 2)
            dve.sem_inc(ln_scaled, 2)
            dve.sem_inc(ln_done, 2)
            dve.sem_inc(hid_ready, len(FF_TILES))
            dve.sem_inc(f_done, 2)
            barrier(dve, 1)
            dve.wait_ge(in_const, 16 * CONST_LOADS)
            dve.tensor_copy(mask_b[:, :], masks_in[:, 0:NBLK * KEYS])
            dve.tensor_copy(mask_a[:, :], masks_in[:, NBLK * KEYS:])
            dve.tensor_copy(ident_bf[:, :], ident[:, :])
            layer_norm(0, N)
            barrier(dve, 2)
            dve.wait_ge(in_a, 16 * A_LOADS)
            pipeline(dve, step_a)
            barrier(dve, 3)
            layer_norm(1, None, add_run=0)
            barrier(dve, 4)
            layer_norm(2, Y)
            over(dve, ffn_over)
            with dve.Fori(0, LAYERS) as L:
                dve.wait_ge(ffn_over, 3 * L + 3)
                pipeline(dve, lambda *a: step_b(NBLK * L, *a))
                over(dve, attn_over)
                layer_norm(L + 3, N, affine=True, L=L)
                over(dve, norm_over)
                feed_forward(L)
                over(dve, ffn_over)
            dve.wait_ge(ffn_over, 3 * LAYERS + 3)
            layer_norm(3 + LAYERS, None, add_run=1)

        @block.tensor
        def _(pe):
            def layer_norm(run, L=None):
                with pe.Fori(0, NCHUNK // 2) as k:
                    if L is not None:
                        pe.wait_ge(attn_over, 4 * L + 4)
                        pe.wait_ge(in_ffn, 48 * L + 48)
                    for h in range(2):
                        n = NCHUNK * run + 2 * k + h
                        pe.wait_ge(ln_staged, 2 * n + 2)
                        pe.wait_ge(ln_scaled, n + 1)
                        pe.matmul(pj[h][:, :], center[:, :], ln_x[:, h, :], start=True,
                                  stop=True).then_inc(ln_centered, 1)
                    for h in range(2):
                        n = NCHUNK * run + 2 * k + h
                        pe.wait_ge(ln_squared, n + 1)
                        pe.wait_ge(ln_rooted, n + 1)
                        pe.matmul(tr[h][:, :], mean_of[:, :], ln_sq[:, h, :], start=True,
                                  stop=True).then_inc(ln_var, 1)

            def step_a(s, par, front, mid, back, since):
                if front:
                    pe.wait_ge(a_staged, 2 * s + 2)
                    if since >= 1:
                        pe.wait_ge(a_qk_copied, s)
                    ones = a_valid[:, par, WIN:WIN + BLK]
                    pe.matmul(pj[0][:, 0:BLK], a_w[:, 0:128], a_x[:, par, WIN:WIN + BLK], start=True, stop=False)
                    pe.matmul(pj[0][:, 0:BLK], a_bias[:, 0:128], ones, start=False, stop=True)
                    pe.matmul(pj[0][:, BLK:BLK + 192], a_w[:, 128:256], a_x[:, par, :], start=True, stop=False)
                    pe.matmul(pj[0][:, BLK:BLK + 192], a_bias[:, 128:256], a_valid[:, par, :], start=False,
                              stop=True).then_inc(a_qk_ready, 1)

                def turn(j):
                    if j == 0:
                        pe.wait_ge(a_exp_done, 4 * s - 4)
                    if j >= 2 or since >= 3:
                        pe.wait_ge(a_pT_copied, 4 * s + j - 9)
                    for p in range(4):
                        last = pe.transpose(tr[j % 2][:, p * P:(p + 1) * P], a_p[:, 4 * j + p, :], ident[:, :])
                    last.then_inc(a_pT_ready, 1)

                def scores(j):
                    w, half = j // 2, j % 2
                    if half == 0:
                        pe.wait_ge(a_q_ready, 2 * s + w - 1)
                    if j >= 2 or since >= 2:
                        pe.wait_ge(a_exp_done, 4 * s + j - 5)
                    bank = sc[j % 2]
                    pe.matmul(bank[:, :], ident_bf[:, :], mask_a[:, :].unsqueeze(1).broadcast_to([P, 4, KEYS_A]),
                              start=True, stop=False, skip_group_check=True)
                    for p in range(4):
                        for a in range(2):
                            head = 2 * (4 * half + p) + a
                            last = pe.matmul(bank[64 * a:64 * a + 64, p * KEYS_A:(p + 1) * KEYS_A],
                                             a_q[:, head, HALF * w:HALF * w + HALF],
                                             a_qk[:, 1 - par, BLK + HALF * w:BLK + HALF * w + KEYS_A],
                                             start=False, stop=True,
                                             skip_group_check=True)
                    last.then_inc(a_scored, 1)

                if back:
                    turn(0)
                    turn(1)
                if mid:
                    scores(0)
                    scores(1)
                if back:
                    turn(2)
                    turn(3)
                    pe.wait_ge(a_pT_copied, 4 * s - 4)
                    pe.wait_ge(a_v_copied, s - 1)
                    if since >= 3:
                        pe.wait_ge(a_o_scaled, s - 2)
                    for w in range(2):
                        for p in range(PAIRS):
                            for a in range(2):
                                col = 64 * w + 8 * p
                                head = 2 * p + a
                                last = pe.matmul(po[64 * a:64 * a + 64, col:col + 8],
                                                 pT[:, 8 * w + p, 64 * a:64 * a + 64],
                                                 a_v[:, par, w, 8 * head:8 * head + 8], start=True, stop=True)
                    last.then_inc(a_pv_done, 1)
                if mid:
                    scores(2)
                    if since >= 2:
                        pe.wait_ge(a_v_copied, s - 1)
                    for w in range(2):
                        out = pj[1][:, P * w:P * w + P]
                        pe.matmul(out, a_x[:, 1 - par, HALF * w:HALF * w + KEYS_A], a_w[:, 256:384], start=True,
                                  stop=False)
                        last = pe.matmul(out, a_valid[:, 1 - par, HALF * w:HALF * w + KEYS_A], a_bias[:, 256:384],
                                         start=False, stop=True)
                    last.then_inc(a_v_ready, 1)
                if back:
                    pe.wait_ge(a_o_scaled, s - 1)
                    if since >= 3:
                        pe.wait_ge(a_y_done, s - 2)
                    pe.transpose(py[:, 256:384], a_on.rearrange("p w n -> p (w n)"), ident[:, :]).then_inc(a_oT_ready, 1)
                if mid:
                    scores(3)
                if back:
                    pe.wait_ge(a_oT_copied, s - 1)
                    for w in range(2):
                        for a in range(2):
                            last = pe.matmul(py[:, HALF * w:HALF * w + HALF], a_wo[:, 2 * w + a, :],
                                             a_oT[:, 64 * a:64 * a + 64], start=(a == 0), stop=(a == 1))
                    last.then_inc(a_y_ready, 1)

            def step_b(base, s, par, front, mid, back, since):
                g = base + s

                def project(n):
                    if n >= 2:
                        pe.wait_ge(qk_copied, 4 * g + n - 1)
                    elif since >= 2:
                        pe.wait_ge(v_copied, 4 * g + n - 5)
                    pe.matmul(pj[n % 2][:, :], xs[:, par, WIN:WIN + BLK], wqkv[:, 512 * n:512 * n + 512],
                              start=True, stop=True).then_inc(qk_ready, 1)

                def turn(n):
                    pe.wait_ge(t1_ready, 4 * g + n - 3)
                    pe.wait_ge(t2_ready, 4 * g + n - 3)
                    if n >= 2:
                        pe.wait_ge(qkT_copied, 4 * g + n - 5)
                    elif since >= 3:
                        pe.wait_ge(pT_copied, 4 * g + n - 9)
                    for p in range(4):
                        out = tr[n % 2][:, p * P:(p + 1) * P]
                        pe.matmul(out, t1[:, n, p * P:(p + 1) * P], ident[:, :], is_transpose=True,
                                  start=True, stop=False)
                        last = pe.matmul(out, t2[:, n, p * P:(p + 1) * P], ident[:, :], is_transpose=True,
                                         start=False, stop=True)
                    last.then_inc(qkT_ready, 1)

                def turn_p(j):
                    pe.wait_ge(p_scaled, 4 * g + j - 7)
                    if j < 2 and mid:
                        pe.wait_ge(qkT_copied, 4 * g + j - 1)
                    else:
                        pe.wait_ge(pT_copied, 4 * g + j - 9)
                    for p in range(4):
                        last = pe.transpose(tr[j % 2][0:KEYS, p * P:(p + 1) * P], pr[:, 4 * j + p, :], ident[:, :])
                    last.then_inc(pT_ready, 1)

                def scores(j):
                    w, half = j // 2, j % 2
                    if j == 0:
                        pe.wait_ge(qkT_copied, 4 * g)
                    if j >= 2 or since >= 2:
                        pe.wait_ge(exp_done, 4 * g + j - 5)
                    bank = sc[j % 2]
                    at = (s - 1) * KEYS if w == 0 else KEYS
                    mask = mask_b[:, bass.ds(at, KEYS)].unsqueeze(1).broadcast_to([P, 4, KEYS])
                    pe.matmul(bank[:, 0:4 * KEYS], ident_bf[:, :], mask, start=True, stop=False,
                              skip_group_check=True)
                    for p in range(4):
                        for a in range(2):
                            rows = slice(64 * a, 64 * a + 64)
                            last = pe.matmul(bank[rows, p * KEYS:(p + 1) * KEYS],
                                             qT[rows, 4 * half + p, HALF * w:HALF * w + HALF],
                                             kW[rows, 1 - par, 4 * half + p, HALF * w:HALF * w + KEYS],
                                             start=False, stop=True, skip_group_check=True)
                    last.then_inc(scored, 1)

                def head_outputs(w):
                    pe.wait_ge(pT_copied, 4 * g + 2 * w - 6)
                    pe.wait_ge(v_copied, 4 * g + 2 * w - 6)
                    if w == 1 or since >= 3:
                        pe.wait_ge(o_copied, 2 * g + w - 4)
                    for p in range(PAIRS):
                        for a in range(2):
                            head = 2 * p + a
                            last = pe.matmul(po[64 * a:64 * a + 64, HALF * p:HALF * p + HALF],
                                             vW[0:KEYS, par, w, DH * head:DH * head + DH],
                                             pT[0:KEYS, PAIRS * w + p, 64 * a:64 * a + 64], start=True, stop=True)
                    last.then_inc(pv_done, 1)

                def values(w):
                    for h in range(2):
                        n = 2 * w + h
                        if n < 2 and front:
                            pe.wait_ge(qk_copied, 4 * g + n + 3)
                        else:
                            pe.wait_ge(v_copied, 4 * g + n - 5)
                        at = 2 * INNER + 512 * h
                        pe.matmul(pj[h][0:KEYS, :], xs[:, 1 - par, HALF * w:HALF * w + KEYS],
                                  wqkv[:, at:at + 512], start=True, stop=True).then_inc(v_ready, 1)

                if front:
                    pe.wait_ge(xs_ready, 2 * g + 2)
                for n in (0, 2):
                    if front:
                        project(n)
                        project(n + 1)
                    if mid:
                        turn(n)
                        turn(n + 1)
                if back:
                    turn_p(0)
                    turn_p(1)
                if mid:
                    scores(0)
                    scores(1)
                if back:
                    turn_p(2)
                    turn_p(3)
                for w in range(2):
                    if mid:
                        values(w)
                        scores(2 + w)
                    if back:
                        head_outputs(w)
                if back:
                    pe.wait_ge(o_copied, 2 * g - 2)
                    if since >= 3:
                        pe.wait_ge(y_done, g - 2)
                    for p in range(PAIRS):
                        last = pe.matmul(py[:, 0:BLK], wo[:, p, :], oT[:, p, :], start=(p == 0),
                                         stop=(p == PAIRS - 1))
                    last.then_inc(y_ready, 1)

            def feed_forward(L):
                with pe.Fori(0, NCHUNK // 2) as k:
                    pe.wait_ge(norm_over, 4 * L + 4)
                    for h in range(2):
                        c = 2 * k + h
                        n = NCHUNK * L + c
                        x = N[:, bass.ds(chunk_col(c), CHUNK)]
                        for t, (at, m) in enumerate(FF_TILES):
                            pe.wait_ge(gelu_done, 3 * n + t + 1)
                            pe.matmul(gate_banks[t][0:m, :], w1[:, FF + at:FF + at + m], x, start=True,
                                      stop=True).then_inc(h_ready, 1)
                            pe.wait_ge(hid_ready, 3 * n + t + 1)
                            pe.matmul(linear_banks[t][0:m, :], w1[:, at:at + m], x, start=True,
                                      stop=True).then_inc(h_ready, 1)
                    for h in range(2):
                        n = NCHUNK * L + 2 * k + h
                        pe.wait_ge(hid_ready, 3 * n + 6)
                        pe.wait_ge(f_done, n + 1)
                        for t, (_, m) in enumerate(FF_TILES):
                            last = pe.matmul((po, py)[h][:, :], w2[0:m, t, :], hid[h][0:m, t, :], start=(t == 0),
                                             stop=(t == len(FF_TILES) - 1))
                        last.then_inc(f_ready, 1)

            pe.sem_inc(ln_centered, 2)
            pe.sem_inc(ln_var, 2)
            barrier(pe, 1)
            pe.wait_ge(in_const, 16 * CONST_LOADS)
            layer_norm(0)
            barrier(pe, 2)
            pe.wait_ge(in_a, 16 * A_LOADS)
            pipeline(pe, step_a)
            barrier(pe, 3)
            layer_norm(1)
            barrier(pe, 4)
            layer_norm(2)
            over(pe, ffn_over)
            with pe.Fori(0, LAYERS) as L:
                pe.wait_ge(ffn_over, 3 * L + 3)
                pe.wait_ge(in_attn, 48 * L + 48)
                pipeline(pe, lambda *a: step_b(NBLK * L, *a))
                over(pe, attn_over)
                layer_norm(L + 3, L)
                over(pe, norm_over)
                feed_forward(L)
                over(pe, ffn_over)
            pe.wait_ge(ffn_over, 3 * LAYERS + 3)
            layer_norm(3 + LAYERS)


def shape_constants():
    f = np.float32
    half = np.arange(0, DH, 2, dtype=f)
    inv_freq = f(1.0) / f(10000.0) ** (half / f(DH))
    t = np.arange(SEQ, dtype=f)
    freqs = t[:, None] * inv_freq[None, :]
    freqs = np.concatenate([freqs, freqs], -1)
    base = (half + f(0.4 * DH)) / f(1.4 * DH)
    power = (t - SEQ // 2) / f(WIN // 2)
    scale = (base[None, :].astype(np.float64) ** power[:, None].astype(np.float64)).astype(f)
    scale = np.concatenate([scale, scale], -1)
    cos, sin = np.cos(freqs), np.sin(freqs)
    sign = np.where(np.arange(DH) < DH // 2, f(-1), f(1))
    tab = np.stack([cos * scale, sign * sin * scale, cos / scale, sign * sin / scale], 1)
    tab = tab.reshape(PER_BATCH, BLK, 4 * DH).transpose(1, 0, 2).reshape(P, PER_BATCH * 4 * DH)

    q = np.arange(P)[:, None] % HALF
    key = np.arange(KEYS)[None, :]
    inner = (key >= q) & (key <= q + WIN)
    first = inner & (key >= WIN)
    mask_b = np.stack([first if i % PER_BATCH == 0 else inner for i in range(NBLK)], 1).reshape(P, -1)
    key_a = np.arange(KEYS_A)[None, :]
    mask_a = (key_a >= q) & (key_a <= q + 2 * WIN)
    valid = np.zeros((1, WIDTH), f)
    for b in range(BATCH):
        at = PAD + b * (PAD + SEQ)
        valid[0, at:at + SEQ] = 1
    masks = np.concatenate([mask_b, mask_a], 1)
    return {
        "tab": np.ascontiguousarray(tab, f),
        "masks": np.where(masks, 0.0, -1e30).astype(f),
        "center": (np.eye(P) - 1.0 / P).astype(f),
        "mean_of": np.full((P, P), 1.0 / P, f),
        "ident": np.eye(P, dtype=f),
        "keep": np.tile((np.arange(1, NBLK + 1) % PER_BATCH != 0).astype(f), (P, 1)),
        "eps_col": np.full((P, 1), EPS_LN, f),
        "a_heads": (np.arange(P)[:, None] // 8 == np.arange(HEADS)[None, :]).astype(f),
        "a_ok": valid,
    }


def laid_out(v):
    x = v["L0_attn_hidden_states"].transpose(2, 0, 1).reshape(E, BATCH * SEQ)
    rows = [np.concatenate([v["L0_attn_q_b"], v["L0_attn_k_b"], v["L0_attn_v_b"]])[None, :]]
    by_parity = v["L0_attn_o_w"].T.reshape(PAIRS, 2, 8, E).transpose(1, 0, 2, 3).reshape(2, 64, E)
    o_t = np.zeros((2, 2, P, E), np.float32)
    for w in range(2):
        o_t[w, :, 64 * w:64 * w + 64] = by_parity
    qs, ks = v["L0_ffn_q_scale"], v["L0_ffn_k_scale"]
    swap = lambda a: np.concatenate([a[:, DH // 2:], a[:, :DH // 2]], 1)
    b1, w2 = v["L0_ffn_b1"], v["L0_ffn_W2"]
    vec = np.zeros((LAYERS, P, 9), np.float32)
    for t, (at, m) in enumerate(FF_TILES):
        vec[:, 0:m, t] = b1[:, FF + at:FF + at + m]
        vec[:, 0:m, 3 + t] = b1[:, at:at + m]
    vec[:, :, 6], vec[:, :, 7], vec[:, :, 8] = v["L0_ffn_b2"], v["L0_ffn_ln_g"], v["L0_ffn_ln_b"]
    w2_rows = np.zeros((LAYERS, len(FF_TILES) * P, E), np.float32)
    w2_rows[:, :FF] = w2
    return {
        "x": x,
        "a_w": np.concatenate([v["L0_attn_q_w"].T, v["L0_attn_k_w"].T, v["L0_attn_v_w"].T], 1),
        "a_wo": o_t.reshape(4, P, E),
        "a_bias": rows[0],
        "a_ob": v["L0_attn_o_b"][:, None],
        "wqkv": v["L0_ffn_Wqkv"],
        "wo": v["L0_ffn_Wo"],
        "w1": v["L0_ffn_W1"],
        "w2": w2_rows,
        "vec": vec,
        "qk_scales": np.concatenate([qs, swap(qs), ks, swap(ks)], 1),
    }


def kernel(**inputs):
    import concourse.bacc as bacc
    from concourse.bass_utils import run_bass_kernel_spmd

    arrays = {**laid_out({k: np.asarray(a) for k, a in inputs.items()}), **shape_constants()}
    arrays = {k: np.ascontiguousarray(a) for k, a in arrays.items()}
    nc = bacc.Bacc("TRN2", target_bir_lowering=False, num_devices=1)
    d = {k: nc.dram_tensor("in_" + k, a.shape, mybir.dt.from_np(a.dtype), kind="ExternalInput").ap()
         for k, a in arrays.items()}
    d["out"] = nc.dram_tensor("out", (E, BATCH * SEQ), F32, kind="ExternalOutput").ap()
    program(nc, d)
    got = run_bass_kernel_spmd(nc, [{"in_" + k: a for k, a in arrays.items()}], core_ids=[0]).results[0]["out"]
    return np.ascontiguousarray(np.asarray(got).reshape(E, BATCH, SEQ).transpose(1, 2, 0))
```

```python
from contextlib import ExitStack

import numpy as np
import concourse.bass as bass
from concourse import mybir

F32 = mybir.dt.float32
F32R = mybir.dt.float32r
BF16 = mybir.dt.bfloat16
I32 = mybir.dt.int32
ACT = mybir.ActivationFunctionType
ALU = mybir.AluOpType
AX_X = mybir.AxisListType.X

P = 128
BATCH, SEQ, E = 2, 2048, 128
LAYERS, HEADS, DH = 6, 16, 64
INNER = HEADS * DH
PARTS = 3 * INNER // 512
FF = 341
WIN = 32
BLK = 128
NBLK = BATCH * SEQ // BLK
PER_BATCH = SEQ // BLK
PAD = WIN + 1
WIDTH = BATCH * (PAD + SEQ) + WIN
CHUNK = 512
NCHUNK = BATCH * SEQ // CHUNK
TURN = 4
HALF = 64
KEYS = WIN + HALF
KEYS_A = WIN + HALF + WIN
PAIRS = HEADS // 2
FF_TILES = [(0, 128), (128, 128), (256, FF - 256)]
QK_SCALE = 8.0
SCALE_A = 8.0 ** -0.5
STEPS = NBLK + 2
EPS_LN = 1e-5
CONST_LOADS = BATCH + 9
A_LOADS = 6
NORM_FLOOR = 1e-24
RSQRT_MAGIC = 0x5F3759DF


def block_col(i):
    return PAD + BLK * i + PAD * (i // PER_BATCH)


def chunk_col(c):
    return PAD + CHUNK * c + PAD * (c // (SEQ // CHUNK))


def pipeline(eng, step):
    step(0, 0, True, False, False, 0)
    step(1, 1, True, True, False, 1)
    with eng.Fori(0, (NBLK - 2) // 2) as k:
        step(2 * k + 2, 0, True, True, True, 2)
        step(2 * k + 3, 1, True, True, True, 3)
    step(NBLK, 0, False, True, True, NBLK)
    step(NBLK + 1, 1, False, False, True, NBLK + 1)


def program(nc, d):
    with ExitStack() as ctx:
        def sb(name, shape, dt=F32):
            return ctx.enter_context(nc.sbuf_tensor(name, shape, dt))

        def psum(name, shape):
            return ctx.enter_context(nc.psum_tensor(name, shape, F32))

        def sem(name):
            return ctx.enter_context(nc.semaphore(name))

        X = sb("X", [P, WIDTH])
        N = sb("N", [P, WIDTH])
        Y = sb("Y", [P, WIDTH])
        Y2 = sb("Y2", [P, WIDTH])
        tab = sb("tab", [P, PER_BATCH * 4 * DH])
        center = sb("center", [P, P])
        center_halves = sb("center_halves", [P, 2 * P])
        mean_of = sb("mean_of", [P, 1])
        all_ones = sb("all_ones", [P, P])
        ident = sb("ident", [P, P])
        ident_bf = sb("ident_bf", [P, P], BF16)
        mask_b = sb("mask_b", [P, 2 * KEYS], BF16)
        mask_a = sb("mask_a", [P, KEYS_A], BF16)
        eps_col = sb("eps_col", [P, 1])
        one_col = sb("one_col", [P, 1])
        keep = sb("keep", [P, NBLK])
        w_hi = sb("w_hi", [P, 3 * INNER], F32R)
        w_lo = sb("w_lo", [P, 3 * INNER], F32R)
        w_raw = X[:, 0:3 * INNER]
        wo = sb("wo", [P, PAIRS, P])
        w1 = sb("w1", [P, 2 * FF])
        w2 = sb("w2", [P, len(FF_TILES), P])
        vec = sb("vec", [P, 9])
        qk_scales = sb("qk_scales", [P, 4 * DH])
        xs_hi = sb("xs_hi", [P, 2, WIN + BLK], F32R)
        xs_lo = sb("xs_lo", [P, 2, WIN + BLK], F32R)
        ts = sb("ts", [P, 2, 4, DH])
        u = sb("u", [P, 4, 512])
        sq = sb("sq", [P, 4, 512])
        t1 = sb("t1", [P, 4, 512])
        t2 = sb("t2", [P, 4, 512])
        ss = sb("ss", [P, 4, 8])
        rn = sb("rn", [P, 4, 8])
        rt = sb("rt", [P, 4, 8])
        qT = sb("qT", [P, PAIRS, BLK])
        kW = sb("kW", [P, 2, PAIRS, WIN + BLK])
        pr = sb("pr", [P, 2 * PAIRS, KEYS])
        pT = sb("pT", [P, 2 * PAIRS, P])
        vW = sb("vW", [P, 2, 2, INNER])
        oT = sb("oT", [P, PAIRS, BLK])
        mx = sb("mx", [P, 16])
        nbias = sb("nbias", [P, 16])
        rsum = sb("rsum", [P, 16])
        rrec = sb("rrec", [P, 16])
        a_room = kW[:, :, :, :].rearrange("p b h n -> p (b h n)")
        a_w = a_room[:, 0:384]
        a_wo = a_room[:, 384:896].rearrange("p (a n) -> p a n", a=4)
        a_bias = a_room[0:1, 896:1280]
        a_ob = a_room[:, 1280:1281]
        a_heads = a_room[:, 1282:1298]
        a_x = t2[:, 0, 0:384].rearrange("p (b n) -> p b n", b=2)
        a_valid = t2[0:1, 1, 0:384].rearrange("p (b n) -> p b n", b=2)
        a_ok = Y[0:1, 0:WIDTH]
        a_q = u[:, :, :].rearrange("p a (b n) -> p (a b) n", n=BLK)
        a_qk = oT[:, :, :].rearrange("p a n -> p (a n)")[:, 0:2 * (BLK + 192)].rearrange("p (b n) -> p b n", b=2)
        a_v = t2[:, 3, 0:512].rearrange("p (b w n) -> p b w n", b=2, w=2)
        a_p = t1[:, :, :].rearrange("p a (b n) -> p (a b) n", n=KEYS_A)
        a_on = sq[:, 0, 0:128].rearrange("p (w n) -> p w n", w=2)
        a_oT = sq[:, 1, 0:128]
        masks_in = vW[:, :, :, :].rearrange("p b w n -> p (b w n)")[:, 0:2 * KEYS + KEYS_A]
        ln_sq = sq
        ln_diag = t1
        ln_r = t2
        ln_o = pT[:, :, :].rearrange("p (b a) n -> p b (a n)", b=TURN)
        ln_sd = sb("ln_sd", [P, 2, 8])
        ln_rs = sb("ln_rs", [P, 2, 8])
        gelu = (u, sq)
        hid = (t1, t2)

        pj = [psum("pj0", [P, 512]), psum("pj1", [P, 512])]
        tr = [psum("tr0", [P, 512]), psum("tr1", [P, 512])]
        sc = [psum("sc0", [P, 512]), psum("sc1", [P, 512])]
        po = psum("po", [P, 512])
        py = psum("py", [P, 512])

        ln_banks = (pj[0], pj[1], sc[0], sc[1])
        ln_var_banks = (po, py)
        gate_banks = (pj[0], tr[0], sc[0])
        linear_banks = (pj[1], tr[1], sc[1])

        bar = sem("bar")
        attn_over = sem("attn_over")
        norm_over = sem("norm_over")
        ffn_over = sem("ffn_over")
        in_const = sem("in_const")
        in_a = sem("in_a")
        in_attn = sem("in_attn")
        in_ffn = sem("in_ffn")
        in_w = sem("in_w")
        w_split = sem("w_split")
        x_out = sem("x_out")
        x_back = sem("x_back")
        zeroed = sem("zeroed")
        stored = sem("stored")
        ln_centered = sem("ln_centered")
        ln_squared = sem("ln_squared")
        ln_var = sem("ln_var")
        ln_rooted = sem("ln_rooted")
        ln_rec = sem("ln_rec")
        ln_diag_ready = sem("ln_diag_ready")
        ln_spread = sem("ln_spread")
        ln_r_ready = sem("ln_r_ready")
        ln_scaled = sem("ln_scaled")
        ln_done = sem("ln_done")
        a_staged = sem("a_staged")
        a_qk_ready = sem("a_qk_ready")
        a_qk_copied = sem("a_qk_copied")
        a_q_ready = sem("a_q_ready")
        a_v_ready = sem("a_v_ready")
        a_v_copied = sem("a_v_copied")
        a_scored = sem("a_scored")
        a_max_chain = sem("a_max_chain")
        a_max_ready = sem("a_max_ready")
        a_exp_done = sem("a_exp_done")
        a_pT_ready = sem("a_pT_ready")
        a_pT_copied = sem("a_pT_copied")
        a_pv_done = sem("a_pv_done")
        a_rec_ready = sem("a_rec_ready")
        a_o_scaled = sem("a_o_scaled")
        a_oT_ready = sem("a_oT_ready")
        a_oT_copied = sem("a_oT_copied")
        a_y_ready = sem("a_y_ready")
        a_y_done = sem("a_y_done")
        xs_ready = sem("xs_ready")
        ts_ready = sem("ts_ready")
        qk_ready = sem("qk_ready")
        qk_copied = sem("qk_copied")
        sq_ready = sem("sq_ready")
        ss_ready = sem("ss_ready")
        rn_chain = sem("rn_chain")
        un_ready = sem("un_ready")
        t1_ready = sem("t1_ready")
        t2_ready = sem("t2_ready")
        rotated = sem("rotated")
        qkT_ready = sem("qkT_ready")
        qkT_copied = sem("qkT_copied")
        v_ready = sem("v_ready")
        v_copied = sem("v_copied")
        scored = sem("scored")
        max_chain = sem("max_chain")
        max_ready = sem("max_ready")
        exp_done = sem("exp_done")
        rec_ready = sem("rec_ready")
        p_scaled = sem("p_scaled")
        pT_ready = sem("pT_ready")
        pT_copied = sem("pT_copied")
        pv_done = sem("pv_done")
        o_copied = sem("o_copied")
        y_ready = sem("y_ready")
        y_done = sem("y_done")
        h_ready = sem("h_ready")
        gelu_done = sem("gelu_done")
        hid_ready = sem("hid_ready")
        f_ready = sem("f_ready")
        f_done = sem("f_done")

        def barrier(eng, k):
            eng.drain().then_inc(bar, 1)
            eng.wait_ge(bar, 4 * k)

        def over(eng, phase):
            eng.drain().then_inc(phase, 1)

        block = ctx.enter_context(nc.Block())

        @block.sync
        def _(sp):
            for b in range(BATCH):
                at = PAD + b * (PAD + SEQ)
                sp.dma_start(X[:, at:at + SEQ], d["x"][:, b * SEQ:(b + 1) * SEQ]).then_inc(in_const, 16)
            for dst, src in ((center, "center"), (center_halves, "center_halves"), (mean_of, "mean_of"), (all_ones, "all_ones"), (ident, "ident"), (masks_in, "masks"),
                             (eps_col, "eps_col"), (keep, "keep")):
                sp.dma_start(dst[:, :], d[src]).then_inc(in_const, 16)
            sp.wait_ge(zeroed, 1)
            for dst, src in ((a_w, "a_w"), (a_bias, "a_bias"), (a_ob, "a_ob"), (a_heads, "a_heads"), (a_ok, "a_ok")):
                sp.dma_start(dst, d[src]).then_inc(in_a, 16)
            sp.dma_start(a_wo, d["a_wo"].rearrange("a p n -> p a n")).then_inc(in_a, 16)
            sp.dma_start(tab[:, :], d["tab"]).then_inc(in_const, 16)

            def load_ffn(n):
                sp.dma_start(w1[:, :], d["w1"][n]).then_inc(in_ffn, 16)
                sp.dma_start(w2[:, :, :], d["w2"][n].rearrange("(t p) n -> p t n", p=P)).then_inc(in_ffn, 16)
                sp.dma_start(vec[:, :], d["vec"][n]).then_inc(in_ffn, 16)

            def load_w(n):
                sp.dma_start(w_raw, d["wqkv"][n]).then_inc(in_w, 16)

            def load_attn(n):
                sp.dma_start(wo[:, :, :], d["wo"][n].rearrange("(t p) n -> p t n", p=P)).then_inc(in_attn, 16)
                sp.dma_start(qk_scales[:, :], d["qk_scales"][n].partition_broadcast(P)).then_inc(in_attn, 16)

            load_ffn(0)
            sp.wait_ge(bar, 4 * 3)
            load_attn(0)
            sp.wait_ge(ln_done, NCHUNK + TURN)
            for b in range(BATCH):
                at = PAD + b * (PAD + SEQ)
                sp.dma_start(d["x_kept"][:, b * SEQ:(b + 1) * SEQ], X[:, at:at + SEQ]).then_inc(x_out, 16)
            sp.wait_ge(x_out, 16 * BATCH)
            sp.wait_ge(ln_centered, 3 * NCHUNK + TURN)
            load_w(0)
            with sp.Fori(0, LAYERS - 1) as n:
                sp.wait_ge(w_split, 2 * PARTS * n + 2 * PARTS)
                load_w(n + 1)
                sp.wait_ge(attn_over, 4 * n + 4)
                load_attn(n + 1)
                sp.wait_ge(ffn_over, 3 * n + 6)
                load_ffn(n + 1)
            sp.wait_ge(w_split, 2 * PARTS * LAYERS)
            for b in range(BATCH):
                at = PAD + b * (PAD + SEQ)
                sp.dma_start(X[:, at:at + SEQ], d["x_kept"][:, b * SEQ:(b + 1) * SEQ]).then_inc(x_back, 16)
            sp.wait_ge(ln_done, 2 * NCHUNK + TURN)
            for b in range(BATCH):
                at = PAD + b * (PAD + SEQ)
                sp.dma_start(d["out"][:, b * SEQ:(b + 1) * SEQ], X[:, at:at + SEQ]).then_inc(stored, 16)
            sp.wait_ge(stored, 16 * BATCH)

        @block.gpsimd
        def _(pool):
            def add_to_x(run, add_run):
                with pool.Fori(0, NCHUNK // TURN) as k:
                    for q in range(TURN):
                        c = TURN * k + q
                        at = chunk_col(c)
                        pool.wait_ge(ln_scaled, NCHUNK * run + c + TURN + 1)
                        pool.tensor_tensor(X[:, bass.ds(at, CHUNK)], X[:, bass.ds(at, CHUNK)], ln_o[:, q, :],
                                           ALU.add).then_inc(ln_done, 1)

            def step_a(s, par, front, mid, back, since):
                if front:
                    at = block_col(s) - WIN
                    if since >= 2:
                        pool.wait_ge(a_v_ready, s - 1)
                    pool.tensor_copy(a_x[:, par, :], N[:, bass.ds(at, KEYS_A + HALF)]).then_inc(a_staged, 1)
                    pool.tensor_copy(a_valid[:, par, :], a_ok[:, bass.ds(at, KEYS_A + HALF)]).then_inc(a_staged, 1)

            def split_weights(L):
                for part in range(2):
                    for n in range(PARTS):
                        at = slice(512 * n, 512 * n + 512)
                        if part == 0:
                            pool.tensor_tensor(w_hi[:, at], w_raw[:, at], one_col[:, 0:1].broadcast_to([P, 512]),
                                               ALU.mult).then_inc(w_split, 1)
                        else:
                            pool.wait_ge(w_split, 2 * PARTS * L + n + 1)
                            pool.tensor_tensor(w_lo[:, at], w_raw[:, at], w_hi[:, at],
                                               ALU.subtract).then_inc(w_split, 1)
                pool.drain()

            def step_b(base, s, par, front, mid, back, since):
                g = base + s

                def normalise(j):
                    pool.wait_ge(rec_ready, 4 * g + j - 7)
                    pool.tensor_tensor(pr[:, 4 * j:4 * j + 4, :], pr[:, 4 * j:4 * j + 4, :],
                                       rrec[:, 4 * j:4 * j + 4].unsqueeze(2).broadcast_to([P, 4, KEYS]),
                                       ALU.mult).then_inc(p_scaled, 1)

                def rotate(n):
                    pool.wait_ge(t2_ready, 4 * g + n - 3)
                    pool.wait_ge(t1_ready, 4 * g + n - 3)
                    pool.tensor_tensor(t1[:, n, :], t1[:, n, :], t2[:, n, :], ALU.add).then_inc(rotated, 1)

                if front:
                    at = block_col(s) - WIN
                    if since >= 2:
                        pool.wait_ge(v_ready, 4 * g - 4)
                    if since >= 1:
                        pool.wait_ge(t1_ready, 4 * g)
                    top = Y[0:64, bass.ds(at, WIN + BLK)]
                    late = Y[64:128, bass.ds(at - 1, WIN + BLK)]
                    ones = one_col[:, 0:1].broadcast_to([P, WIN + BLK])
                    pool.tensor_tensor(xs_hi[0:64, par, :], top, ones[0:64, :], ALU.mult).then_inc(xs_ready, 1)
                    pool.tensor_tensor(xs_hi[64:128, par, :], late, ones[64:128, :], ALU.mult).then_inc(xs_ready, 1)
                    pool.drain()
                    pool.tensor_tensor(xs_lo[0:64, par, :], top, xs_hi[0:64, par, :],
                                       ALU.subtract).then_inc(xs_ready, 1)
                    pool.tensor_tensor(xs_lo[64:128, par, :], late, xs_hi[64:128, par, :],
                                       ALU.subtract).then_inc(xs_ready, 1)
                    pool.wait_ge(xs_ready, 4 * g + 4)
                if mid:
                    for n in range(4):
                        rotate(n)
                if back:
                    normalise(0)
                    normalise(1)
                    normalise(2)
                    normalise(3)
                if front:
                    if since >= 2:
                        pool.wait_ge(t2_ready, 4 * g - 4)
                    pool.tensor_tensor(ts[:, par, :, :].rearrange("p t d -> p (t d)"),
                                       tab[:, bass.ds((s % PER_BATCH) * 4 * DH, 4 * DH)],
                                       qk_scales[:, :], ALU.mult).then_inc(ts_ready, 1)
                    pool.wait_ge(ts_ready, g + 1)
                    for n in range(4):
                        pool.wait_ge(un_ready, 4 * g + n + 1)
                        if since >= 1:
                            pool.wait_ge(qkT_ready, 4 * g + n - 3)
                        table = ts[:, par, 2 * (n // 2), :].unsqueeze(1).broadcast_to([P, 8, DH])
                        pool.tensor_tensor(t1[:, n, :].rearrange("p (h d) -> p h d", d=DH),
                                           u[:, n, :].rearrange("p (h d) -> p h d", d=DH), table,
                                           ALU.mult).then_inc(t1_ready, 1)

            pool.memset(one_col[:, :], 1.0)
            pool.memset(N[:, :], 0.0)
            pool.memset(Y2[:, :], 0.0)
            barrier(pool, 1)
            pool.wait_ge(in_const, 16 * CONST_LOADS)
            barrier(pool, 2)
            pool.wait_ge(in_a, 16 * A_LOADS)
            pipeline(pool, step_a)
            barrier(pool, 3)
            pool.memset(kW[:, 0, :, 0:WIN], 0.0)
            add_to_x(1, 0)
            barrier(pool, 4)
            with pool.Fori(0, LAYERS) as L:
                pool.wait_ge(in_w, 16 * L + 16)
                split_weights(L)
                pool.wait_ge(ffn_over, 3 * L + 3)
                pool.wait_ge(in_attn, 32 * L + 32)
                pipeline(pool, lambda *a: step_b(NBLK * L, *a))
                over(pool, attn_over)
                over(pool, norm_over)
            pool.wait_ge(ffn_over, 3 * LAYERS + 3)
            pool.wait_ge(x_back, 16 * BATCH)
            add_to_x(3 + LAYERS, 1)

        @block.scalar
        def _(act):
            def layer_norm(run, L=None):
                with act.Fori(0, NCHUNK // TURN) as k:
                    if L is not None:
                        act.wait_ge(attn_over, 4 * L + 4)
                    for q in range(TURN):
                        n = NCHUNK * run + TURN * k + q
                        act.wait_ge(ln_centered, n + TURN + 1)
                        act.wait_ge(ln_var, n + 1)
                        act.activation(ln_sq[:, q, :], ln_banks[q][:, :], ACT.Square).then_inc(ln_squared, 1)
                    for h in range(2):
                        pair = (NCHUNK * run + TURN * k) // 2 + h
                        act.wait_ge(ln_var, 2 * pair + TURN + 2)
                        act.wait_ge(ln_rec, pair + 1)
                        act.activation(ln_sd[:, h, :], ln_var_banks[h][:, 0:8], ACT.Sqrt,
                                       bias=eps_col[:, 0:1]).then_inc(ln_rooted, 1)

            def step_a(s, par, front, mid, back, since):
                def turned(j):
                    act.wait_ge(a_pT_ready, 4 * s + j - 7)
                    act.copy(pT[:, 4 * j:4 * j + 4, :].rearrange("p a n -> p (a n)"),
                             tr[j % 2][:, :]).then_inc(a_pT_copied, 1)

                def exponentials(j):
                    act.wait_ge(a_max_ready, 4 * s + j - 3)
                    for p in range(4):
                        last = act.activation(a_p[:, 4 * j + p, :], sc[j % 2][:, p * KEYS_A:(p + 1) * KEYS_A],
                                              ACT.Exp, bias=nbias[:, 4 * j + p:4 * j + p + 1], scale=SCALE_A,
                                              accum_out=rsum[:, 4 * j + p:4 * j + p + 1])
                    last.then_inc(a_exp_done, 1)

                if front:
                    act.wait_ge(a_qk_ready, s + 1)
                    act.copy(a_qk[:, par, :], pj[0][:, 0:BLK + 192]).then_inc(a_qk_copied, 1)
                if back:
                    turned(0)
                    turned(1)
                if mid:
                    if since >= 2:
                        act.wait_ge(a_rec_ready, s - 1)
                    exponentials(0)
                if back:
                    turned(2)
                    turned(3)
                if mid:
                    exponentials(1)
                    act.wait_ge(a_v_ready, s)
                    act.copy(a_v[:, 1 - par, :, :].rearrange("p w n -> p (w n)"),
                             pj[1][:, 0:256]).then_inc(a_v_copied, 1)
                    exponentials(2)
                if back:
                    act.wait_ge(a_oT_ready, s - 1)
                    act.copy(a_oT, py[:, 256:384]).then_inc(a_oT_copied, 1)
                if mid:
                    exponentials(3)
                if back:
                    act.wait_ge(a_y_ready, s - 1)
                    act.activation(Y2[:, bass.ds(block_col(s - 2), BLK)], py[:, 0:BLK], ACT.Identity,
                                   bias=a_ob).then_inc(a_y_done, 1)

            def step_b(base, s, par, front, mid, back, since):
                g = base + s

                def projected(n):
                    act.wait_ge(qk_ready, 4 * g + n + 1)
                    if since >= 1:
                        act.wait_ge(t1_ready, 4 * g + n - 3)
                        act.wait_ge(t2_ready, 4 * g + n - 3)
                    act.copy(u[:, n, :], pj[n % 2][:, :])
                    act.activation(sq[:, n, :], pj[n % 2][:, :], ACT.Square).then_inc(qk_copied, 1)

                def turned(n):
                    act.wait_ge(qkT_ready, 4 * g + n - 3)
                    bank = tr[n % 2][:, :].rearrange("p (a n) -> p a n", n=BLK)
                    half = 4 * (n % 2)
                    if n < 2:
                        last = act.copy(qT[:, half:half + 4, :], bank)
                    else:
                        act.copy(kW[:, 1 - par, half:half + 4, WIN:WIN + BLK], bank)
                        last = act.activation(kW[:, par, half:half + 4, 0:WIN], bank[:, :, BLK - WIN:BLK],
                                              ACT.Identity, scale=keep[:, bass.ds(s - 1, 1)])
                    last.then_inc(qkT_copied, 1)

                def turned_p(j):
                    act.wait_ge(pT_ready, 4 * g + j - 7)
                    act.copy(pT[0:KEYS, 4 * j:4 * j + 4, :].rearrange("p a n -> p (a n)"),
                             tr[j % 2][0:KEYS, :]).then_inc(pT_copied, 1)

                def exponentials(j):
                    act.wait_ge(max_ready, 4 * g + j - 3)
                    for p in range(4):
                        last = act.activation(pr[:, 4 * j + p, :], sc[j % 2][:, p * KEYS:(p + 1) * KEYS],
                                              ACT.Exp, bias=nbias[:, 4 * j + p:4 * j + p + 1], scale=QK_SCALE,
                                              accum_out=rsum[:, 4 * j + p:4 * j + p + 1])
                    last.then_inc(exp_done, 1)

                def outputs(w):
                    act.wait_ge(pv_done, 2 * g + w - 3)
                    act.copy(oT[:, :, HALF * w:HALF * w + HALF],
                             po[:, :].rearrange("p (a n) -> p a n", n=HALF)).then_inc(o_copied, 1)

                for n in (0, 2):
                    if front:
                        projected(n)
                        projected(n + 1)
                    if mid:
                        turned(n)
                        turned(n + 1)
                if back:
                    turned_p(0)
                    turned_p(1)
                    turned_p(2)
                if mid:
                    exponentials(0)
                if back:
                    turned_p(3)
                if mid:
                    exponentials(1)
                for w in range(2):
                    if back:
                        outputs(w)
                    if mid:
                        exponentials(2 + w)

            def feed_forward(L):
                with act.Fori(0, NCHUNK // 2) as k:
                    act.wait_ge(norm_over, 4 * L + 4)
                    for h in range(2):
                        n = NCHUNK * L + 2 * k + h
                        for t, (_, m) in enumerate(FF_TILES):
                            act.wait_ge(h_ready, 6 * n + 2 * t + 1)
                            act.activation(gelu[h][0:m, t, :], gate_banks[t][0:m, :], ACT.Gelu,
                                           bias=vec[0:m, t:t + 1]).then_inc(gelu_done, 1)

            act.sem_inc(ln_rooted, 2)
            act.sem_inc(gelu_done, len(FF_TILES))
            barrier(act, 1)
            act.wait_ge(in_const, 16 * CONST_LOADS)
            layer_norm(0)
            barrier(act, 2)
            act.wait_ge(in_a, 16 * A_LOADS)
            pipeline(act, step_a)
            barrier(act, 3)
            layer_norm(1)
            barrier(act, 4)
            layer_norm(2)
            over(act, ffn_over)
            with act.Fori(0, LAYERS) as L:
                act.wait_ge(ffn_over, 3 * L + 3)
                pipeline(act, lambda *a: step_b(NBLK * L, *a))
                over(act, attn_over)
                layer_norm(L + 3, L)
                over(act, norm_over)
                feed_forward(L)
                over(act, ffn_over)
            act.wait_ge(ffn_over, 3 * LAYERS + 3)
            layer_norm(3 + LAYERS)

        @block.vector
        def _(dve):
            def layer_norm(run, dst, affine=False, add_run=None, L=None):
                with dve.Fori(0, NCHUNK // TURN) as k:
                    if L is not None:
                        dve.wait_ge(attn_over, 4 * L + 4)
                        dve.wait_ge(in_ffn, 48 * L + 48)
                    for h in range(2):
                        pair = (NCHUNK * run + TURN * k) // 2 + h
                        dve.wait_ge(ln_rooted, pair + 3)
                        dve.reciprocal(ln_rs[:, h, :], ln_sd[:, h, :]).then_inc(ln_rec, 1)
                        dve.wait_ge(ln_rec, pair + 3)
                        for q in (2 * h, 2 * h + 1):
                            dve.wait_ge(ln_spread, NCHUNK * run + TURN * k + q + 1)
                            cols = slice(4 * (q % 2), 4 * (q % 2) + 4)
                            dve.tensor_tensor(ln_diag[:, q, :].rearrange("p (b n) -> p b n", n=P),
                                              ident[:, :].unsqueeze(1).broadcast_to([P, 4, P]),
                                              ln_rs[:, h, cols].unsqueeze(2).broadcast_to([P, 4, P]),
                                              ALU.mult).then_inc(ln_diag_ready, 1)
                    for q in range(TURN):
                        c = TURN * k + q
                        n = NCHUNK * run + c
                        at = chunk_col(c)
                        if add_run is not None:
                            dve.wait_ge(ln_done, NCHUNK * add_run + c + 1)
                        dve.wait_ge(ln_spread, n + TURN + 1)
                        dve.tensor_copy(ln_r[:, q % 2, :], tr[q % 2][:, :]).then_inc(ln_r_ready, 1)
                        out = ln_o[:, q, :] if affine or add_run is not None else dst[:, bass.ds(at, CHUNK)]
                        dve.wait_ge(ln_r_ready, n + 1)
                        dve.tensor_tensor(out, ln_banks[q][:, :], ln_r[:, q % 2, :], ALU.mult).then_inc(ln_scaled, 1)
                        if affine:
                            dve.wait_ge(ln_scaled, n + TURN + 1)
                            dve.tensor_scalar(dst[:, bass.ds(at, CHUNK)], ln_o[:, q, :], vec[:, 7:8], vec[:, 8:9],
                                              ALU.mult, ALU.add)

            def step_a(s, par, front, mid, back, since):
                def maxima(j):
                    dve.wait_ge(a_scored, 4 * s + j - 3)
                    dve.reduce_max(mx[:, 4 * j:4 * j + 4], sc[j % 2][:, :].rearrange("p (a n) -> p a n", n=KEYS_A),
                                   axis=AX_X).then_inc(a_max_chain, 1)
                    dve.wait_ge(a_max_chain, 4 * s + j - 3)
                    dve.tensor_scalar(nbias[:, 4 * j:4 * j + 4], mx[:, 4 * j:4 * j + 4], -SCALE_A, None,
                                      ALU.mult).then_inc(a_max_ready, 1)

                def spread(w):
                    at = slice(HALF * w, HALF * w + HALF)
                    dve.tensor_tensor(a_q[:, :, at], a_qk[:, par, at].unsqueeze(1).broadcast_to([P, HEADS, HALF]),
                                      a_heads.unsqueeze(2).broadcast_to([P, HEADS, HALF]),
                                      ALU.mult).then_inc(a_q_ready, 1)

                if back:
                    dve.wait_ge(a_exp_done, 4 * s - 4)
                    dve.reciprocal(rrec[:, :], rsum[:, :]).then_inc(a_rec_ready, 1)
                if mid:
                    maxima(0)
                    maxima(1)
                if front:
                    dve.wait_ge(a_qk_copied, s + 1)
                    spread(0)
                if back:
                    dve.wait_ge(a_pv_done, s - 1)
                    dve.wait_ge(a_rec_ready, s - 1)
                    dve.tensor_tensor(a_on.rearrange("p w (a d) -> p (w a) d", d=8),
                                      po[:, 0:128].rearrange("p (a d) -> p a d", d=8),
                                      rrec[:, :].unsqueeze(2).broadcast_to([P, 16, 8]),
                                      ALU.mult).then_inc(a_o_scaled, 1)
                if mid:
                    maxima(2)
                    maxima(3)
                if front:
                    spread(1)

            CHAIN = 12

            def step_b(base, s, par, front, mid, back, since):
                g = base + s

                def values(n):
                    dve.wait_ge(v_ready, 4 * g + n - 3)
                    dve.tensor_copy(vW[0:KEYS, 1 - par, n // 2, 512 * (n % 2):512 * (n % 2) + 512],
                                    pj[n % 2][0:KEYS, :]).then_inc(v_copied, 1)

                def second_term(n):
                    dve.wait_ge(un_ready, 4 * g + n + 1)
                    if since >= 1:
                        dve.wait_ge(qkT_ready, 4 * g + n - 3)
                    if n == 0:
                        dve.wait_ge(ts_ready, g + 1)
                    src = u[:, n, :].rearrange("p (h d) -> p h d", d=DH)
                    dst = t2[:, n, :].rearrange("p (h d) -> p h d", d=DH)
                    table = ts[:, par, 2 * (n // 2) + 1, :].unsqueeze(1).broadcast_to([P, 8, DH])
                    dve.tensor_tensor(dst[:, :, 0:32], src[:, :, 32:64], table[:, :, 0:32], ALU.mult)
                    dve.tensor_tensor(dst[:, :, 32:64], src[:, :, 0:32], table[:, :, 32:64],
                                      ALU.mult).then_inc(t2_ready, 1)

                def maxima(j):
                    dve.wait_ge(scored, 4 * g + j - 3)
                    dve.reduce_max(mx[:, 4 * j:4 * j + 4],
                                   sc[j % 2][:, 0:4 * KEYS].rearrange("p (a n) -> p a n", n=KEYS),
                                   axis=AX_X).then_inc(max_chain, 1)
                    dve.wait_ge(max_chain, 4 * g + j - 3)
                    dve.tensor_scalar(nbias[:, 4 * j:4 * j + 4], mx[:, 4 * j:4 * j + 4], -QK_SCALE, None,
                                      ALU.mult).then_inc(max_ready, 1)

                def sums(j):
                    dve.wait_ge(exp_done, 4 * g + j - 3)
                    dve.reciprocal(rrec[:, 4 * j:4 * j + 4], rsum[:, 4 * j:4 * j + 4]).then_inc(rec_ready, 1)

                if front:
                    for n in range(4):
                        dve.wait_ge(qk_copied, 4 * g + n + 1)
                        dve.reduce_sum(ss[:, n, :], sq[:, n, :].rearrange("p (h d) -> p h d", d=DH),
                                       axis=AX_X).then_inc(ss_ready, 1)
                    all_ss = ss[:, :, :].rearrange("p a b -> p (a b)")
                    y = rn[:, :, :].rearrange("p a b -> p (a b)")
                    t = rt[:, :, :].rearrange("p a b -> p (a b)")
                    dve.wait_ge(ss_ready, 4 * g + 4)
                    dve.tensor_scalar(all_ss, all_ss, NORM_FLOOR, None, ALU.max).then_inc(rn_chain, 1)
                    dve.wait_ge(rn_chain, CHAIN * g + 1)
                    dve.tensor_scalar(t.bitcast(I32), all_ss.bitcast(I32), 1, None,
                                      ALU.logical_shift_right).then_inc(rn_chain, 1)
                    dve.wait_ge(rn_chain, CHAIN * g + 2)
                    dve.tensor_scalar(y.bitcast(I32), t.bitcast(I32), -1.0, float(RSQRT_MAGIC), ALU.mult,
                                      ALU.add).then_inc(rn_chain, 1)
                    for r in range(3):
                        dve.wait_ge(rn_chain, CHAIN * g + 3 * r + 3)
                        dve.scalar_tensor_tensor(t, y, -0.5, y, ALU.mult, ALU.mult).then_inc(rn_chain, 1)
                        dve.wait_ge(rn_chain, CHAIN * g + 3 * r + 4)
                        dve.tensor_tensor(t, t, all_ss, ALU.mult).then_inc(rn_chain, 1)
                        if mid:
                            if r < 2:
                                values(r)
                            else:
                                maxima(0)
                        dve.wait_ge(rn_chain, CHAIN * g + 3 * r + 5)
                        dve.scalar_tensor_tensor(y, t, 1.5, y, ALU.add, ALU.mult).then_inc(rn_chain, 1)
                    dve.wait_ge(rn_chain, CHAIN * g + CHAIN)
                if mid and not front:
                    values(0)
                    values(1)
                for n in range(4):
                    if front:
                        dve.tensor_tensor(u[:, n, :].rearrange("p (h d) -> p h d", d=DH),
                                          u[:, n, :].rearrange("p (h d) -> p h d", d=DH),
                                          rn[:, n, :].unsqueeze(2).broadcast_to([P, 8, DH]),
                                          ALU.mult).then_inc(un_ready, 1)
                    if mid and (n == 1 or n == 0 and not front):
                        maxima(n)
                if mid:
                    values(2)
                    values(3)
                    maxima(2)
                if front:
                    second_term(0)
                if front:
                    second_term(1)
                if mid:
                    sums(0)
                    sums(1)
                    maxima(3)
                if front:
                    second_term(2)
                    second_term(3)
                if mid:
                    sums(2)
                    sums(3)
                if back:
                    at = block_col(s - 2)
                    dve.wait_ge(y_ready, g - 1)
                    dve.tensor_tensor(Y2[:, bass.ds(at, BLK)], py[:, 0:BLK], Y[:, bass.ds(at, BLK)],
                                      ALU.add).then_inc(y_done, 1)

            def feed_forward(L):
                with dve.Fori(0, NCHUNK // 2) as k:
                    dve.wait_ge(norm_over, 4 * L + 4)
                    for h in range(2):
                        n = NCHUNK * L + 2 * k + h
                        for t, (_, m) in enumerate(FF_TILES):
                            dve.wait_ge(h_ready, 6 * n + 2 * t + 2)
                            dve.wait_ge(gelu_done, 3 * n + t + 4)
                            dve.scalar_tensor_tensor(hid[h][0:m, t, :], linear_banks[t][0:m, :],
                                                     vec[0:m, 3 + t:4 + t], gelu[h][0:m, t, :],
                                                     ALU.add, ALU.mult).then_inc(hid_ready, 1)
                    for h in range(2):
                        c = 2 * k + h
                        at = chunk_col(c)
                        dve.wait_ge(f_ready, NCHUNK * L + c + 1)
                        dve.scalar_tensor_tensor(Y[:, bass.ds(at, CHUNK)], (po, py)[h][:, :], vec[:, 6:7],
                                                 Y2[:, bass.ds(at, CHUNK)], ALU.add, ALU.add).then_inc(f_done, 1)

            dve.memset(Y[:, :], 0.0).then_inc(zeroed, 1)
            dve.sem_inc(ln_rec, 2)
            dve.sem_inc(ln_scaled, TURN)
            dve.sem_inc(ln_done, TURN)
            dve.sem_inc(hid_ready, len(FF_TILES))
            dve.sem_inc(f_done, 2)
            barrier(dve, 1)
            dve.wait_ge(in_const, 16 * CONST_LOADS)
            dve.tensor_copy(mask_b[:, :], masks_in[:, 0:2 * KEYS])
            dve.tensor_copy(mask_a[:, :], masks_in[:, 2 * KEYS:])
            dve.tensor_copy(ident_bf[:, :], ident[:, :])
            layer_norm(0, N)
            barrier(dve, 2)
            dve.wait_ge(in_a, 16 * A_LOADS)
            pipeline(dve, step_a)
            barrier(dve, 3)
            layer_norm(1, None, add_run=0)
            barrier(dve, 4)
            layer_norm(2, Y)
            over(dve, ffn_over)
            with dve.Fori(0, LAYERS) as L:
                dve.wait_ge(ffn_over, 3 * L + 3)
                pipeline(dve, lambda *a: step_b(NBLK * L, *a))
                over(dve, attn_over)
                layer_norm(L + 3, N, affine=True, L=L)
                over(dve, norm_over)
                feed_forward(L)
                over(dve, ffn_over)
            dve.wait_ge(ffn_over, 3 * LAYERS + 3)
            layer_norm(3 + LAYERS, None, add_run=1)

        @block.tensor
        def _(pe):
            def layer_norm(src, run, L=None):
                with pe.Fori(0, NCHUNK // TURN) as k:
                    if L is not None:
                        pe.wait_ge(attn_over, 4 * L + 4)
                    for q in range(TURN):
                        n = NCHUNK * run + TURN * k + q
                        at = chunk_col(TURN * k + q)
                        pe.wait_ge(ln_scaled, n + 1)
                        if L is None:
                            last = pe.matmul(ln_banks[q][:, :], center[:, :], src[:, bass.ds(at, CHUNK)],
                                             start=True, stop=True)
                        else:
                            pe.matmul(ln_banks[q][:, :], center_halves[:, 0:P], src[:, bass.ds(at, CHUNK)],
                                      start=True, stop=False)
                            last = pe.matmul(ln_banks[q][:, :], center_halves[:, P:2 * P],
                                             src[:, bass.ds(at - 1, CHUNK)], start=False, stop=True)
                        last.then_inc(ln_centered, 1)
                    for q in range(TURN):
                        n = NCHUNK * run + TURN * k + q
                        pe.wait_ge(ln_squared, n + 1)
                        if q % 2 == 0:
                            pe.wait_ge(ln_rooted, (NCHUNK * run + TURN * k) // 2 + q // 2 + 1)
                        for b in range(4):
                            col = 4 * (q % 2) + b
                            last = pe.matmul(ln_var_banks[q // 2][:, col:col + 1], ln_sq[:, q, b * P:(b + 1) * P],
                                             mean_of[:, 0:1], start=True, stop=True)
                        last.then_inc(ln_var, 1)
                    for q in range(TURN):
                        n = NCHUNK * run + TURN * k + q
                        pe.wait_ge(ln_diag_ready, n + 1)
                        pe.wait_ge(ln_scaled, n + 3)
                        pe.matmul(tr[q % 2][:, :], all_ones[:, :], ln_diag[:, q, :], start=True,
                                  stop=True).then_inc(ln_spread, 1)

            def step_a(s, par, front, mid, back, since):
                if front:
                    pe.wait_ge(a_staged, 2 * s + 2)
                    if since >= 1:
                        pe.wait_ge(a_qk_copied, s)
                    ones = a_valid[:, par, WIN:WIN + BLK]
                    pe.matmul(pj[0][:, 0:BLK], a_w[:, 0:128], a_x[:, par, WIN:WIN + BLK], start=True, stop=False)
                    pe.matmul(pj[0][:, 0:BLK], a_bias[:, 0:128], ones, start=False, stop=True)
                    pe.matmul(pj[0][:, BLK:BLK + 192], a_w[:, 128:256], a_x[:, par, :], start=True, stop=False)
                    pe.matmul(pj[0][:, BLK:BLK + 192], a_bias[:, 128:256], a_valid[:, par, :], start=False,
                              stop=True).then_inc(a_qk_ready, 1)

                def turn(j):
                    if j == 0:
                        pe.wait_ge(a_exp_done, 4 * s - 4)
                    if j >= 2 or since >= 3:
                        pe.wait_ge(a_pT_copied, 4 * s + j - 9)
                    for p in range(4):
                        last = pe.transpose(tr[j % 2][:, p * P:(p + 1) * P], a_p[:, 4 * j + p, :], ident[:, :])
                    last.then_inc(a_pT_ready, 1)

                def scores(j):
                    w, half = j // 2, j % 2
                    if half == 0:
                        pe.wait_ge(a_q_ready, 2 * s + w - 1)
                    if j >= 2 or since >= 2:
                        pe.wait_ge(a_exp_done, 4 * s + j - 5)
                    bank = sc[j % 2]
                    pe.matmul(bank[:, :], ident_bf[:, :], mask_a[:, :].unsqueeze(1).broadcast_to([P, 4, KEYS_A]),
                              start=True, stop=False, skip_group_check=True)
                    for p in range(4):
                        for a in range(2):
                            head = 2 * (4 * half + p) + a
                            last = pe.matmul(bank[64 * a:64 * a + 64, p * KEYS_A:(p + 1) * KEYS_A],
                                             a_q[:, head, HALF * w:HALF * w + HALF],
                                             a_qk[:, 1 - par, BLK + HALF * w:BLK + HALF * w + KEYS_A],
                                             start=False, stop=True,
                                             skip_group_check=True)
                    last.then_inc(a_scored, 1)

                if back:
                    turn(0)
                    turn(1)
                if mid:
                    scores(0)
                    scores(1)
                if back:
                    turn(2)
                    turn(3)
                if mid:
                    if since >= 2:
                        pe.wait_ge(a_v_copied, s - 1)
                    for w in range(2):
                        out = pj[1][:, P * w:P * w + P]
                        pe.matmul(out, a_x[:, 1 - par, HALF * w:HALF * w + KEYS_A], a_w[:, 256:384], start=True,
                                  stop=False)
                        last = pe.matmul(out, a_valid[:, 1 - par, HALF * w:HALF * w + KEYS_A], a_bias[:, 256:384],
                                         start=False, stop=True)
                    last.then_inc(a_v_ready, 1)
                if back:
                    pe.wait_ge(a_pT_copied, 4 * s - 4)
                    pe.wait_ge(a_v_copied, s - 1)
                    if since >= 3:
                        pe.wait_ge(a_o_scaled, s - 2)
                    for w in range(2):
                        for p in range(PAIRS):
                            for a in range(2):
                                col = 64 * w + 8 * p
                                head = 2 * p + a
                                last = pe.matmul(po[64 * a:64 * a + 64, col:col + 8],
                                                 pT[:, 8 * w + p, 64 * a:64 * a + 64],
                                                 a_v[:, par, w, 8 * head:8 * head + 8], start=True, stop=True)
                    last.then_inc(a_pv_done, 1)
                if mid:
                    scores(2)
                if back:
                    pe.wait_ge(a_o_scaled, s - 1)
                    if since >= 3:
                        pe.wait_ge(a_y_done, s - 2)
                    pe.transpose(py[:, 256:384], a_on.rearrange("p w n -> p (w n)"), ident[:, :]).then_inc(a_oT_ready, 1)
                if mid:
                    scores(3)
                if back:
                    pe.wait_ge(a_oT_copied, s - 1)
                    for w in range(2):
                        for a in range(2):
                            last = pe.matmul(py[:, HALF * w:HALF * w + HALF], a_wo[:, 2 * w + a, :],
                                             a_oT[:, 64 * a:64 * a + 64], start=(a == 0), stop=(a == 1))
                    last.then_inc(a_y_ready, 1)

            def step_b(base, s, par, front, mid, back, since):
                g = base + s

                def three_products(out, buf, tokens, at):
                    cols = slice(at, at + 512)
                    pe.matmul(out, xs_hi[:, buf, tokens], w_hi[:, cols], start=True, stop=False)
                    pe.matmul(out, xs_hi[:, buf, tokens], w_lo[:, cols], start=False, stop=False)
                    return pe.matmul(out, xs_lo[:, buf, tokens], w_hi[:, cols], start=False, stop=True)

                def project(n):
                    if n >= 2:
                        pe.wait_ge(qk_copied, 4 * g + n - 1)
                    elif since >= 2:
                        pe.wait_ge(v_copied, 4 * g + n - 5)
                    three_products(pj[n % 2][:, :], par, slice(WIN, WIN + BLK), 512 * n).then_inc(qk_ready, 1)

                def turn(n):
                    pe.wait_ge(rotated, 4 * g + n - 3)
                    if n >= 2:
                        pe.wait_ge(qkT_copied, 4 * g + n - 5)
                    elif since >= 3:
                        pe.wait_ge(pT_copied, 4 * g + n - 9)
                    for p in range(4):
                        last = pe.transpose(tr[n % 2][:, p * P:(p + 1) * P], t1[:, n, p * P:(p + 1) * P],
                                            ident[:, :])
                    last.then_inc(qkT_ready, 1)

                def turn_p(j):
                    pe.wait_ge(p_scaled, 4 * g + j - 7)
                    if j < 2 and mid:
                        pe.wait_ge(qkT_copied, 4 * g + j - 1)
                    else:
                        pe.wait_ge(pT_copied, 4 * g + j - 9)
                    for p in range(4):
                        last = pe.transpose(tr[j % 2][0:KEYS, p * P:(p + 1) * P], pr[:, 4 * j + p, :], ident[:, :])
                    last.then_inc(pT_ready, 1)

                def scores(j):
                    w, half = j // 2, j % 2
                    if j == 0:
                        pe.wait_ge(qkT_copied, 4 * g)
                    if j >= 2 or since >= 2:
                        pe.wait_ge(exp_done, 4 * g + j - 5)
                    bank = sc[j % 2]
                    inner = ((s - 1) % PER_BATCH + PER_BATCH - 1) // PER_BATCH if w == 0 else 1
                    at = inner * KEYS
                    mask = mask_b[:, bass.ds(at, KEYS)].unsqueeze(1).broadcast_to([P, 4, KEYS])
                    pe.matmul(bank[:, 0:4 * KEYS], ident_bf[:, :], mask, start=True, stop=False,
                              skip_group_check=True)
                    for p in range(4):
                        for a in range(2):
                            rows = slice(64 * a, 64 * a + 64)
                            last = pe.matmul(bank[rows, p * KEYS:(p + 1) * KEYS],
                                             qT[rows, 4 * half + p, HALF * w:HALF * w + HALF],
                                             kW[rows, 1 - par, 4 * half + p, HALF * w:HALF * w + KEYS],
                                             start=False, stop=True, skip_group_check=True)
                    last.then_inc(scored, 1)

                def head_outputs(w):
                    pe.wait_ge(pT_copied, 4 * g + 2 * w - 6)
                    pe.wait_ge(v_copied, 4 * g + 2 * w - 6)
                    if w == 1 or since >= 3:
                        pe.wait_ge(o_copied, 2 * g + w - 4)
                    for p in range(PAIRS):
                        for a in range(2):
                            head = 2 * p + a
                            last = pe.matmul(po[64 * a:64 * a + 64, HALF * p:HALF * p + HALF],
                                             vW[0:KEYS, par, w, DH * head:DH * head + DH],
                                             pT[0:KEYS, PAIRS * w + p, 64 * a:64 * a + 64], start=True, stop=True)
                    last.then_inc(pv_done, 1)

                def values(w):
                    for h in range(2):
                        n = 2 * w + h
                        if n < 2 and front:
                            pe.wait_ge(qk_copied, 4 * g + n + 3)
                        else:
                            pe.wait_ge(v_copied, 4 * g + n - 5)
                        at = 2 * INNER + 512 * h
                        three_products(pj[h][0:KEYS, :], 1 - par, slice(HALF * w, HALF * w + KEYS),
                                       at).then_inc(v_ready, 1)

                if front:
                    pe.wait_ge(xs_ready, 4 * g + 4)
                for n in (0, 2):
                    if front:
                        project(n)
                        project(n + 1)
                    if mid:
                        turn(n)
                        turn(n + 1)
                if mid:
                    values(0)
                if back:
                    turn_p(0)
                    turn_p(1)
                if mid:
                    scores(0)
                    scores(1)
                if back:
                    turn_p(2)
                    turn_p(3)
                if mid:
                    values(1)
                    scores(2)
                if back:
                    head_outputs(0)
                if mid:
                    scores(3)
                if back:
                    head_outputs(1)
                    if since >= 3:
                        pe.wait_ge(y_done, g - 2)
                    pe.wait_ge(o_copied, 2 * g - 2)
                    for p in range(PAIRS):
                        last = pe.matmul(py[:, 0:BLK], wo[:, p, :], oT[:, p, :], start=(p == 0),
                                         stop=(p == PAIRS - 1))
                    last.then_inc(y_ready, 1)

            def feed_forward(L):
                with pe.Fori(0, NCHUNK // 2) as k:
                    pe.wait_ge(norm_over, 4 * L + 4)
                    for h in range(2):
                        c = 2 * k + h
                        n = NCHUNK * L + c
                        x = N[:, bass.ds(chunk_col(c), CHUNK)]
                        for t, (at, m) in enumerate(FF_TILES):
                            pe.wait_ge(gelu_done, 3 * n + t + 1)
                            pe.matmul(gate_banks[t][0:m, :], w1[:, FF + at:FF + at + m], x, start=True,
                                      stop=True).then_inc(h_ready, 1)
                            pe.wait_ge(hid_ready, 3 * n + t + 1)
                            pe.matmul(linear_banks[t][0:m, :], w1[:, at:at + m], x, start=True,
                                      stop=True).then_inc(h_ready, 1)
                    for h in range(2):
                        n = NCHUNK * L + 2 * k + h
                        pe.wait_ge(hid_ready, 3 * n + 6)
                        pe.wait_ge(f_done, n + 1)
                        for t, (_, m) in enumerate(FF_TILES):
                            last = pe.matmul((po, py)[h][:, :], w2[0:m, t, :], hid[h][0:m, t, :], start=(t == 0),
                                             stop=(t == len(FF_TILES) - 1))
                        last.then_inc(f_ready, 1)

            pe.sem_inc(ln_centered, TURN)
            pe.sem_inc(ln_var, TURN)
            pe.sem_inc(ln_spread, TURN)
            barrier(pe, 1)
            pe.wait_ge(in_const, 16 * CONST_LOADS)
            layer_norm(X, 0)
            barrier(pe, 2)
            pe.wait_ge(in_a, 16 * A_LOADS)
            pipeline(pe, step_a)
            barrier(pe, 3)
            layer_norm(Y2, 1)
            barrier(pe, 4)
            layer_norm(X, 2)
            over(pe, ffn_over)
            with pe.Fori(0, LAYERS) as L:
                pe.wait_ge(ffn_over, 3 * L + 3)
                pe.wait_ge(in_attn, 32 * L + 32)
                pe.wait_ge(w_split, 2 * PARTS * L + 2 * PARTS)
                pipeline(pe, lambda *a: step_b(NBLK * L, *a))
                over(pe, attn_over)
                layer_norm(Y2, L + 3, L)
                over(pe, norm_over)
                feed_forward(L)
                over(pe, ffn_over)
            pe.wait_ge(ffn_over, 3 * LAYERS + 3)
            layer_norm(Y, 3 + LAYERS)


def shape_constants():
    f = np.float32
    half = np.arange(0, DH, 2, dtype=f)
    inv_freq = f(1.0) / f(10000.0) ** (half / f(DH))
    t = np.arange(SEQ, dtype=f)
    freqs = t[:, None] * inv_freq[None, :]
    freqs = np.concatenate([freqs, freqs], -1)
    base = (half + f(0.4 * DH)) / f(1.4 * DH)
    power = (t - SEQ // 2) / f(WIN // 2)
    scale = (base[None, :].astype(np.float64) ** power[:, None].astype(np.float64)).astype(f)
    scale = np.concatenate([scale, scale], -1)
    cos, sin = np.cos(freqs), np.sin(freqs)
    sign = np.where(np.arange(DH) < DH // 2, f(-1), f(1))
    tab = np.stack([cos * scale, sign * sin * scale, cos / scale, sign * sin / scale], 1)
    tab = tab.reshape(PER_BATCH, BLK, 4 * DH).transpose(1, 0, 2).reshape(P, PER_BATCH * 4 * DH)

    q = np.arange(P)[:, None] % HALF
    key = np.arange(KEYS)[None, :]
    inner = (key >= q) & (key <= q + WIN)
    first = inner & (key >= WIN)
    mask_b = np.concatenate([first, inner], 1)
    key_a = np.arange(KEYS_A)[None, :]
    mask_a = (key_a >= q) & (key_a <= q + 2 * WIN)
    valid = np.zeros((1, WIDTH), f)
    for b in range(BATCH):
        at = PAD + b * (PAD + SEQ)
        valid[0, at:at + SEQ] = 1
    masks = np.concatenate([mask_b, mask_a], 1)
    return {
        "tab": np.ascontiguousarray(tab, f),
        "masks": np.where(masks, 0.0, -1e30).astype(f),
        "center": (np.eye(P) - 1.0 / P).astype(f),
        "center_halves": np.concatenate([(np.eye(P) - 1.0 / P) * (np.arange(P)[:, None] // 64 == h)
                                         for h in range(2)], 1).astype(f),
        "mean_of": np.full((P, 1), 1.0 / P, f),
        "all_ones": np.ones((P, P), f),
        "ident": np.eye(P, dtype=f),
        "keep": np.tile((np.arange(1, NBLK + 1) % PER_BATCH != 0).astype(f), (P, 1)),
        "eps_col": np.full((P, 1), EPS_LN, f),
        "a_heads": (np.arange(P)[:, None] // 8 == np.arange(HEADS)[None, :]).astype(f),
        "a_ok": valid,
    }


def laid_out(v):
    x = v["L0_attn_hidden_states"].transpose(2, 0, 1).reshape(E, BATCH * SEQ)
    rows = [np.concatenate([v["L0_attn_q_b"], v["L0_attn_k_b"], v["L0_attn_v_b"]])[None, :]]
    by_parity = v["L0_attn_o_w"].T.reshape(PAIRS, 2, 8, E).transpose(1, 0, 2, 3).reshape(2, 64, E)
    o_t = np.zeros((2, 2, P, E), np.float32)
    for w in range(2):
        o_t[w, :, 64 * w:64 * w + 64] = by_parity
    qs, ks = v["L0_ffn_q_scale"], v["L0_ffn_k_scale"]
    swap = lambda a: np.concatenate([a[:, DH // 2:], a[:, :DH // 2]], 1)
    b1, w2 = v["L0_ffn_b1"], v["L0_ffn_W2"]
    vec = np.zeros((LAYERS, P, 9), np.float32)
    for t, (at, m) in enumerate(FF_TILES):
        vec[:, 0:m, t] = b1[:, FF + at:FF + at + m]
        vec[:, 0:m, 3 + t] = b1[:, at:at + m]
    vec[:, :, 6], vec[:, :, 7], vec[:, :, 8] = v["L0_ffn_b2"], v["L0_ffn_ln_g"], v["L0_ffn_ln_b"]
    w2_rows = np.zeros((LAYERS, len(FF_TILES) * P, E), np.float32)
    w2_rows[:, :FF] = w2
    return {
        "x": x,
        "a_w": np.concatenate([v["L0_attn_q_w"].T, v["L0_attn_k_w"].T, v["L0_attn_v_w"].T], 1),
        "a_wo": o_t.reshape(4, P, E),
        "a_bias": rows[0],
        "a_ob": v["L0_attn_o_b"][:, None],
        "wqkv": v["L0_ffn_Wqkv"],
        "wo": v["L0_ffn_Wo"],
        "w1": v["L0_ffn_W1"],
        "w2": w2_rows,
        "vec": vec,
        "qk_scales": np.concatenate([qs, swap(qs), ks, swap(ks)], 1),
    }


def kernel(**inputs):
    import concourse.bacc as bacc
    from concourse.bass_utils import run_bass_kernel_spmd

    arrays = {**laid_out({k: np.asarray(a) for k, a in inputs.items()}), **shape_constants()}
    arrays = {k: np.ascontiguousarray(a) for k, a in arrays.items()}
    nc = bacc.Bacc("TRN2", target_bir_lowering=False, num_devices=1)
    d = {k: nc.dram_tensor("in_" + k, a.shape, mybir.dt.from_np(a.dtype), kind="ExternalInput").ap()
         for k, a in arrays.items()}
    d["out"] = nc.dram_tensor("out", (E, BATCH * SEQ), F32, kind="ExternalOutput").ap()
    d["x_kept"] = nc.dram_tensor("x_kept", (E, BATCH * SEQ), F32, kind="Internal").ap()
    program(nc, d)
    got = run_bass_kernel_spmd(nc, [{"in_" + k: a for k, a in arrays.items()}], core_ids=[0]).results[0]["out"]
    return np.ascontiguousarray(np.asarray(got).reshape(E, BATCH, SEQ).transpose(1, 2, 0))
```
